# Optimizing a Trainium2 kernel written in Bass

```python
import numpy as np
import jax
import jax.numpy as jnp

def _softmax(x, axis=-1):
    return jax.nn.softmax(x, axis=axis)

def _gelu(x):
    return jax.nn.gelu(x, approximate=True)

def _silu(x):
    return jax.nn.silu(x)

def _sigmoid(x):
    return jax.nn.sigmoid(x)

def _layernorm(x, axis=-1, eps=1e-05):
    m = jnp.mean(x, axis=axis, keepdims=True)
    v = jnp.var(x, axis=axis, keepdims=True)
    return (x - m) / jnp.sqrt(v + eps)

def _scatter_add(tgt, idx, src, axis=0):
    return tgt.at[idx].add(src)

def _segment_sum(src, seg, n):
    return jax.ops.segment_sum(src, seg, n)
kernel_name = 'mk_macaron_d1_jaxref_r8_0da64a'

def setup_inputs(seed: int=0):
    np.random.seed(seed)
    _w = jnp.asarray

    def _L0_attn_setup():
        import jax, jax.numpy as jnp
        import numpy as np
        BATCH, SEQ, D_EMBED, N_HEADS, D_HEAD = (1, 256, 128, 16, 64)
        MASK_VAL = 10000000000.0
        key = jax.random.key(seed)
        ks = jax.random.split(key, 5)
        s = 1.0 / np.sqrt(D_EMBED).astype(np.float32)
        return {'x': jax.random.normal(ks[0], (BATCH, SEQ, D_EMBED), jnp.float32), 'W_Q': jax.random.normal(ks[1], (N_HEADS, D_HEAD, D_EMBED), jnp.float32) * s, 'W_K': jax.random.normal(ks[2], (N_HEADS, D_HEAD, D_EMBED), jnp.float32) * s, 'W_V': jax.random.normal(ks[3], (N_HEADS, D_HEAD, D_EMBED), jnp.float32) * s, 'W_O': jax.random.normal(ks[4], (N_HEADS, D_EMBED, D_HEAD), jnp.float32) * s}
    _L0_attn_in = _L0_attn_setup()

    def _L0_ffn_setup():
        import jax, jax.numpy as jnp
        import numpy as np
        NEG_INF = jnp.float32(-1000000000.0)

        def _router(x, Wr, br, top_k=2):
            logits = jnp.einsum('bsd,de->bse', x, Wr) + br
            _, top_idx = jax.lax.top_k(logits, top_k)
            num_experts = logits.shape[-1]
            mask = jnp.any(top_idx[..., None] == jnp.arange(num_experts), axis=-2)
            sparse_logits = jnp.where(mask, logits, NEG_INF)
            weights = jax.nn.softmax(sparse_logits, axis=-1)
            return (weights, top_idx, mask)
        key = jax.random.key(seed)
        ks = jax.random.split(key, 8)
        B, S, D, E, H = (4, 256, 128, 8, 512)
        sd = 1.0 / np.sqrt(D)
        sh = 1.0 / np.sqrt(H)
        x = jax.random.normal(ks[0], (B, S, D), dtype=jnp.float32)
        Wr = jax.random.normal(ks[1], (D, E), dtype=jnp.float32) * sd
        br = jnp.zeros((E,), dtype=jnp.float32)
        W1 = jax.random.normal(ks[2], (E, D, H), dtype=jnp.float32) * sd
        b1 = jnp.zeros((E, H), dtype=jnp.float32)
        W2 = jax.random.normal(ks[3], (E, H, D), dtype=jnp.float32) * sh
        b2 = jnp.zeros((E, D), dtype=jnp.float32)
        return {'x': x, 'Wr': Wr, 'br': br, 'W1': W1, 'b1': b1, 'W2': W2, 'b2': b2}
    _L0_ffn_in = _L0_ffn_setup()
    _d = {'L0_attn_x': _L0_attn_in['x'], 'L0_attn_W_Q': _L0_attn_in['W_Q'], 'L0_attn_W_K': _L0_attn_in['W_K'], 'L0_attn_W_V': _L0_attn_in['W_V'], 'L0_attn_W_O': _L0_attn_in['W_O'], 'L0_ffn_Wr': _L0_ffn_in['Wr'], 'L0_ffn_br': _L0_ffn_in['br'], 'L0_ffn_W1': _L0_ffn_in['W1'], 'L0_ffn_b1': _L0_ffn_in['b1'], 'L0_ffn_W2': _L0_ffn_in['W2'], 'L0_ffn_b2': _L0_ffn_in['b2']}
    _x0 = _d['L0_attn_x']
    _d['L0_attn_x'] = jax.random.normal(jax.random.fold_in(jax.random.key(seed), 1), (8, 512, 128), dtype=_x0.dtype)
    del _x0
    return _d

def reference(L0_attn_x, L0_attn_W_Q, L0_attn_W_K, L0_attn_W_V, L0_attn_W_O, L0_ffn_Wr, L0_ffn_br, L0_ffn_W1, L0_ffn_b1, L0_ffn_W2, L0_ffn_b2):

    def _L0_attn_ref(x, W_Q, W_K, W_V, W_O):
        import jax, jax.numpy as jnp
        import numpy as np
        BATCH, SEQ, D_EMBED, N_HEADS, D_HEAD = (1, 256, 128, 16, 64)
        MASK_VAL = 10000000000.0
        q = jnp.einsum('ahe,bce->bach', W_Q, x)
        k = jnp.einsum('ahe,bce->bach', W_K, x)
        v = jnp.einsum('ahe,bce->bach', W_V, x)
        n = x.shape[1]
        scores = jnp.einsum('bach,baCh->bacC', k, q)
        causal = jnp.tril(jnp.ones((n, n), dtype=bool))
        masked = jnp.where(causal, scores, jnp.float32(-MASK_VAL))
        attn = jax.nn.softmax(masked / np.float32(np.sqrt(D_HEAD)), axis=-1)
        z = jnp.einsum('bacC,baCh->bach', attn, v)
        out = jnp.einsum('aeh,bach->bce', W_O, z)
        return out

    def _L0_ffn_ref(x, Wr, br, W1, b1, W2, b2):
        import jax, jax.numpy as jnp
        import numpy as np
        NEG_INF = jnp.float32(-1000000000.0)

        def _router(x, Wr, br, top_k=2):
            logits = jnp.einsum('bsd,de->bse', x, Wr) + br
            _, top_idx = jax.lax.top_k(logits, top_k)
            num_experts = logits.shape[-1]
            mask = jnp.any(top_idx[..., None] == jnp.arange(num_experts), axis=-2)
            sparse_logits = jnp.where(mask, logits, NEG_INF)
            weights = jax.nn.softmax(sparse_logits, axis=-1)
            return (weights, top_idx, mask)
        weights, top_idx, mask = _router(x, Wr, br, top_k=2)
        num_experts = W1.shape[0]
        out = jnp.zeros_like(x)
        for e in range(num_experts):
            h = jax.nn.relu(jnp.einsum('bsd,dh->bsh', x, W1[e]) + b1[e])
            y = jnp.einsum('bsh,hd->bsd', h, W2[e]) + b2[e]
            w = weights[:, :, e] * mask[:, :, e].astype(x.dtype)
            out = out + y * w[:, :, None]
        return out
    x = L0_attn_x
    x = x + 0.5 * _L0_ffn_ref(_layernorm(x, axis=-1), L0_ffn_Wr, L0_ffn_br, L0_ffn_W1, L0_ffn_b1, L0_ffn_W2, L0_ffn_b2)
    x = x + _L0_attn_ref(_layernorm(x, axis=-1), L0_attn_W_Q, L0_attn_W_K, L0_attn_W_V, L0_attn_W_O)
    x = x + 0.5 * _L0_ffn_ref(_layernorm(x, axis=-1), L0_ffn_Wr, L0_ffn_br, L0_ffn_W1, L0_ffn_b1, L0_ffn_W2, L0_ffn_b2)
    return x

_drawn_inputs = setup_inputs


def setup_inputs(seed=0):
    import zlib

    import numpy as np

    out = dict(_drawn_inputs(seed))
    spreads = {'L0_ffn_br': (0.0, 0.1), 'L0_ffn_b1': (0.0, 0.1), 'L0_ffn_b2': (0.0, 0.1)}
    factors = {}
    for name, (base, spread) in spreads.items():
        noise = np.random.default_rng([zlib.crc32(name.encode()), seed]).standard_normal(out[name].shape)
        drawn = base * np.exp(spread * noise) if base else spread * noise
        out[name] = jnp.asarray(drawn.astype(out[name].dtype))
    for name, factor in factors.items():
        out[name] = (out[name] * factor).astype(out[name].dtype)
    return out
```

```python
import concourse.bass as bass
from concourse import mybir
from contextlib import ExitStack


def macaron_block_kernel(
    nc: bass.Bass,
    x: bass.AP,
    w_q: bass.AP,
    w_k: bass.AP,
    w_v: bass.AP,
    w_o: bass.AP,
    w_r: bass.AP,
    b_r: bass.AP,
    w_1: bass.AP,
    b_1: bass.AP,
    w_2: bass.AP,
    b_2: bass.AP,
    out: bass.AP,
):
    fp32 = mybir.dt.float32
    fp32r = mybir.dt.float32r
    bf16 = mybir.dt.bfloat16
    ALU = mybir.AluOpType
    ACT = mybir.ActivationFunctionType
    AX = mybir.AxisListType

    P = 128
    BATCH, SEQ, D = x.shape
    HEADS, DH, _ = w_q.shape
    TILES = BATCH * SEQ // P
    QT = SEQ // P
    PAIRS = HEADS // 2
    STEPS = BATCH * PAIRS
    EXPERTS, _, HIDDEN = w_1.shape
    CHUNKS = HIDDEN // P
    GROUPS = 2
    GB = BATCH // GROUPS
    GT = GB * QT
    TOP = 2
    UNROLL = 4
    SLOT_TILES = -(-((GT * P * TOP + EXPERTS * (P - 1)) // P) // UNROLL) * UNROLL
    assert (SLOT_TILES // UNROLL - 2) * UNROLL == TOP * GT
    assert STEPS // GROUPS == TOP * GT
    RING = 4
    INSTANCES = 2 * GROUPS
    SCALE = float(DH) ** -0.5
    EPS = 1e-5
    MASKED = -1e10

    x_tiles = x.rearrange("b (t p) d -> p (b t) d", p=P)
    out_tiles = out.rearrange("b (t p) d -> p (b t) d", p=P)

    ctx = ExitStack()
    with ctx:
        def sb(name, shape, dt=fp32):
            return ctx.enter_context(nc.sbuf_tensor(name, shape, dt))

        def sem(name):
            return ctx.enter_context(nc.semaphore(name))

        xs = sb("xs", [P, TILES, D])
        ident = sb("ident", [P, P])
        ident_bf = sb("ident_bf", [P, P], bf16)
        causal_bf = sb("causal_bf", [P, P], bf16)
        before_bf = sb("before_bf", [P, P], bf16)
        ones_bf = sb("ones_bf", [P, P], bf16)

        kq = sb("kq", [P, HEADS, 2, D], fp32r)
        wv_t = sb("wv_t", [D, PAIRS * P])
        wo_t = sb("wo_t", [P, PAIRS * D])
        w1_hi = sb("w1_hi", [D, EXPERTS * HIDDEN], fp32r)
        w1_lo = sb("w1_lo", [D, EXPERTS * HIDDEN], fp32r)
        w2_sb = sb("w2_sb", [P, EXPERTS * CHUNKS * D])
        b1_t = sb("b1_t", [P, EXPERTS * CHUNKS])
        b2_bc = sb("b2_bc", [P, EXPERTS, D])
        wr_sb = sb("wr_sb", [D, EXPERTS])
        br_bc = sb("br_bc", [P, EXPERTS])

        arena = sb("arena", [P, 8192])
        used = [0]

        def lot(columns):
            used[0] += columns
            assert used[0] <= 8192
            return arena[:, used[0] - columns:used[0]]

        wk_nat = lot(HEADS * D)[0:DH, :].rearrange("p (a e) -> p a e", a=HEADS)
        wq_nat = lot(HEADS * D)[0:DH, :].rearrange("p (a e) -> p a e", a=HEADS)
        wv_nat = lot(PAIRS * D).rearrange("p (j e) -> p j e", j=PAIRS)
        wo_nat = lot(HEADS * DH).rearrange("p (a h) -> p a h", a=HEADS)
        b1_nat = lot(P)[0:EXPERTS * CHUNKS, :]
        zeros = lot(1024)
        used[0] = 0
        probs = [lot(QT * SEQ).rearrange("p (t k) -> p t k", t=QT) for h in range(2)]
        probs_t = [lot(QT * SEQ).rearrange("p (k t) -> p k t", k=QT) for h in range(2)]
        used[0] = 0
        xg = [lot(D) for i in range(4)]
        h_sb = [lot(HIDDEN) for i in range(2)]
        h_t = [lot(HIDDEN).rearrange("p (c n) -> p c n", c=CHUNKS) for i in range(2)]
        y_sb = [lot(D) for i in range(2)]
        yg = [sb(f"yg{i}", [P, D])[:, :] for i in range(RING)]

        arena2 = sb("arena2", [P, 7 * SEQ])
        used2 = [0]

        def lot2(columns):
            used2[0] += columns
            assert used2[0] <= 7 * SEQ
            return arena2[:, used2[0] - columns:used2[0]]

        xn_st = [lot2(SEQ) for i in range(2)]
        v_sb = [lot2(SEQ).rearrange("p (t m) -> p t m", t=QT) for i in range(2)]
        inv_bc = [lot2(SEQ).rearrange("p (q t) -> p q t", t=QT) for i in range(2)]
        z_sb = lot2(SEQ)
        used2[0] = 0
        xt_r = [lot2(QT * P) for i in range(2)]
        rt = [lot2(GT * EXPERTS).rearrange("p (t e) -> p t e", e=EXPERTS) for i in range(6)]
        rt2 = [lot2(SLOT_TILES * EXPERTS) for i in range(2)]

        w1_raw = sb("w1_raw", [D, EXPERTS * HIDDEN])
        xn_t = w1_raw[:, 0:GT * P]
        xn_all = [sb("xn_all0", [P, GT, D])[:, :, :],
                  w1_raw[:, GT * P:2 * GT * P].rearrange("p (t d) -> p t d", t=GT)]
        xn_hi = sb("xn_hi", [D, GT * P], fp32r)
        xn_lo = sb("xn_lo", [D, GT * P], fp32r)
        bn = sb("bn", [P, GT, 6])
        mean = sb("mean", [P, GT])
        half_var = sb("half_var", [P, GT])
        rstd = sb("rstd", [P, GT])
        ln_t = sb("ln_t", [P, GT])

        rank = sb("rank", [P, EXPERTS])
        tile_start = sb("tile_start", [P, GT])
        upto = sb("upto", [P, EXPERTS, EXPERTS])
        tile_no = sb("tile_no", [P, SLOT_TILES])
        gate = [sb(f"gate{q}", [P, GT, TOP]) for q in range(GROUPS)]
        slot = [sb(f"slot{q}", [P, TOP, GT], mybir.dt.int32) for q in range(GROUPS)]
        expert_of = [sb(f"expert_of{q}", [P, SLOT_TILES], mybir.dt.int32) for q in range(GROUPS)]
        count_bf = sb("count_bf", [P, GT * EXPERTS], bf16)
        top = [sb(f"top{k}", [P, GT]) for k in range(4)]
        ex = sb("ex", [P, 4, EXPERTS])

        kq_st = [sb(f"kq_st{i}", [P, 2, 2, D], fp32r) for i in range(2)]
        g_hi = [sb(f"g_hi{i}", [D, 2, SEQ], fp32r) for i in range(2)]
        g_lo = [sb(f"g_lo{i}", [D, 2, SEQ], fp32r) for i in range(2)]
        xg_hi = [g_hi[i][:, 0, 0:P] for i in range(2)]
        xg_lo = [g_lo[i][:, 0, 0:P] for i in range(2)]
        neg_max = sb("neg_max", [P, 2, QT])
        row_sum = sb("row_sum", [P, 2, QT])
        inv_sum = [sb(f"inv_sum{i}", [P, 2, QT]) for i in range(2)]
        inv_dram = nc.dram_tensor("inv_dram", [2, 2, P, QT], fp32).ap()
        x_slots = [nc.dram_tensor(f"x_slots{q}", [SLOT_TILES * P, D], fp32).ap() for q in range(GROUPS)]
        y_slots = [nc.dram_tensor(f"y_slots{q}", [SLOT_TILES * P, D], fp32).ap() for q in range(GROUPS)]

        bank = [ctx.enter_context(nc.psum_tensor(f"bank{i}", [P, 512], fp32)) for i in range(8)]

        x_loaded = [sem(f"x_loaded{q}") for q in range(GROUPS)]
        w_loaded = sem("w_loaded")
        const_ready = sem("const_ready")
        out_stored = sem("out_stored")

        kq_ps = sem("kq_ps")
        kq_hi_ready = sem("kq_hi_ready")
        kq_lo_ready = sem("kq_lo_ready")
        wt_ps = sem("wt_ps")
        wt_ready = sem("wt_ready")

        chain = sem("chain")
        xn_ready = sem("xn_ready")
        tr_ps = sem("tr_ps")
        tr_taken = sem("tr_taken")
        xnt_done = sem("xnt_done")
        w1_hi_ready = sem("w1_hi_ready")
        w1_lo_ready = sem("w1_lo_ready")
        ffn_w_loaded = sem("ffn_w_loaded")
        router_w_loaded = sem("router_w_loaded")
        zeroed = [sem(f"zeroed{q}") for q in range(GROUPS)]
        w2_loaded = sem("w2_loaded")
        zeros_ready = sem("zeros_ready")

        logits_ps = sem("logits_ps")
        delta_ready = sem("delta_ready")
        exp_delta = sem("exp_delta")
        counts_ready = sem("counts_ready")
        places_ps = sem("places_ps")
        routed = sem("routed")
        scattered = [sem(f"scattered{f}") for f in range(INSTANCES)]
        xg_loaded = [sem(f"xg_loaded{i}") for i in range(4)]
        xgt_ps = sem("xgt_ps")
        xg_hi_ready = sem("xg_hi_ready")
        xg_lo_ready = sem("xg_lo_ready")
        up_ps = sem("up_ps")
        up_ready = sem("up_ready")
        ht_ps = sem("ht_ps")
        ht_ready = sem("ht_ready")
        y_ps = sem("y_ps")
        y_ready = sem("y_ready")
        y_stored = [[sem(f"y_stored{f}_{i}") for i in range(2)] for f in range(INSTANCES)]
        gathered = [[sem(f"gathered{f}_{i}") for i in range(RING)] for f in range(INSTANCES)]
        combined = sem("combined")

        staged = [sem(f"staged{i}") for i in range(2)]
        g_ps = sem("g_ps")
        g_hi_ready = sem("g_hi_ready")
        g_lo_ready = sem("g_lo_ready")
        v_ps = sem("v_ps")
        v_ready = sem("v_ready")
        s_ps = sem("s_ps")
        max_ready = sem("max_ready")
        exp_done = sem("exp_done")
        inv_ready = sem("inv_ready")
        inv_stored = sem("inv_stored")
        inv_loaded = [sem(f"inv_loaded{i}") for i in range(2)]
        pt_ps = sem("pt_ps")
        pt_act = sem("pt_act")
        pt_dve = sem("pt_dve")
        z_ps = sem("z_ps")
        z_ready = sem("z_ready")
        o_ps = sem("o_ps")
        o_added = sem("o_added")

        def wait(engine, semaphore, value):
            if not isinstance(value, int) or value > 0:
                engine.wait_ge(semaphore, value)

        def attention_steps(engine, half, step):
            start, end = half * STEPS // GROUPS, (half + 1) * STEPS // GROUPS
            step(start, 0, True, False)
            step(start + 1, 1, False, False)
            with engine.Fori(start // 2 + 1, end // 2 - 1) as m:
                step(2 * m, 0, False, False)
                step(2 * m + 1, 1, False, False)
            step(end - 2, 0, False, False)
            step(end - 1, 1, False, True)

        def experts_of(engine, q, start, count):
            _, values = nc.values_load_multi_w_load_instructions(
                expert_of[q][0:1, bass.ds(start, count)], engines=[engine], min_val=0, max_val=EXPERTS - 1,
                skip_runtime_bounds_check_because="route() writes a count of experts, clamped to EXPERTS - 1")
            return values

        def ring_of(f):
            return 2 if f == 1 else RING

        def slot_tiles(engine, turn):
            turn(0)
            with engine.Fori(1, SLOT_TILES // UNROLL - 1) as m:
                turn(m)
            turn(SLOT_TILES // UNROLL - 1)

        def tile_of(g, t):
            return xs[:, bass.ds(g * QT + t, 1), :].rearrange("p o d -> p (o d)")

        def seq_of(i, half):
            return i // PAIRS - half * GB

        def pair_of(i):
            return i % PAIRS

        ZERO_FILLS = SLOT_TILES // 8

        keys_of = [max(2 * P, (t + 1) * P) for t in range(QT)]

        S_BANK, J_BANK, T_BANK, ZO_BANK = bank[0:3], bank[3:5], bank[5:7], bank[7]
        S_USE, S_COL, S_USES = [0, 0, 1, 2], [0, 2 * P, 0, 0], 3

        def score_tile(t, columns):
            return S_BANK[S_USE[t]][:, S_COL[t] + columns.start:S_COL[t] + columns.stop]

        block = ctx.enter_context(nc.Block())

        @block.sync
        def _(sp):
            for q in range(GROUPS):
                tiles = slice(q * GT, (q + 1) * GT)
                sp.dma_start(xs[:, tiles, :], x_tiles[:, tiles, :]).then_inc(x_loaded[q], 16)
            sp.dma_start(wk_nat, w_k.rearrange("a h e -> h a e")).then_inc(w_loaded, 16)
            sp.dma_start(wq_nat, w_q.rearrange("a h e -> h a e")).then_inc(w_loaded, 16)
            sp.dma_start(wv_nat, w_v.rearrange("(j a) h e -> (a h) j e", a=2)).then_inc(w_loaded, 16)
            sp.dma_start(wo_nat, w_o.rearrange("a e h -> e a h")).then_inc(w_loaded, 16)

            def slots_io(f):
                q = f % GROUPS
                sp.wait_ge(scattered[f], 16 * TOP * GT)

                def load(n, u):
                    c = f * SLOT_TILES + n
                    wait(sp, xgt_ps, c - 3)
                    sp.dma_start(xg[u % 4], x_slots[q][bass.ds(n * P, P), :]).then_inc(xg_loaded[u % 4], 16)

                def store(n, u):
                    sp.wait_ge(y_ready, f * SLOT_TILES + n + 1)
                    sp.dma_start(y_slots[q][bass.ds(n * P, P), :], y_sb[u % 2]).then_inc(y_stored[f][u % 2], 16)

                for n in range(3):
                    load(n, n)

                def turn(m):
                    for u in range(UNROLL):
                        n = UNROLL * m + u
                        if not (isinstance(m, int) and n < 3):
                            store(n - 3, u + 1)
                        if not (isinstance(m, int) and n + 3 >= SLOT_TILES):
                            load(n + 3, u + 3)

                slot_tiles(sp, turn)
                for n in range(SLOT_TILES - 3, SLOT_TILES):
                    store(n, n)

            def attention_io(half):
                def stage(i, par):
                    wait(sp, g_ps, 2 * (i - 1))
                    wait(sp, v_ps, i - 1)
                    sp.dma_start(kq_st[par][:, :, :, :].bitcast(fp32),
                                 kq[:, bass.ds(pair_of(i) * 2, 2), :, :].bitcast(fp32)).then_inc(staged[par], 16)
                    sp.dma_start(xn_st[par][:, :], xn_t[:, bass.ds(seq_of(i, half) * SEQ, SEQ)]).then_inc(staged[par], 16)

                end = (half + 1) * STEPS // GROUPS

                def step(i, par, first, last):
                    if not (isinstance(i, int) and i + 2 >= end):
                        stage(i + 2, par)
                    sp.wait_ge(inv_ready, 2 * i + 2)
                    sp.dma_start(inv_dram[par].rearrange("h q t -> q h t"), inv_sum[par][:, :, :]).then_inc(inv_stored, 16)
                    sp.wait_ge(inv_stored, 16 * (i + 1))
                    for h in range(2):
                        sp.dma_start(
                            inv_bc[par][h * DH:(h + 1) * DH, :, :],
                            inv_dram[par, h].rearrange("q (o t) -> o q t", o=1).broadcast_to([DH, P, QT]),
                        ).then_inc(inv_loaded[par], 16)

                sp.wait_ge(kq_lo_ready, HEADS // 4)
                sp.wait_ge(xnt_done, GB * half + 1)
                if half > 0:
                    sp.wait_ge(routed, GROUPS + half)
                stage(half * STEPS // GROUPS, 0)
                stage(half * STEPS // GROUPS + 1, 1)
                sp.wait_ge(xnt_done, GB * (half + 1))
                attention_steps(sp, half, step)

            sp.wait_ge(wt_ps, 5)
            for q in range(GROUPS):
                sp.wait_ge(zeroed[q], 16 * ZERO_FILLS)
            slots_io(0)
            slots_io(1)
            attention_io(0)
            attention_io(1)
            sp.wait_ge(o_added, STEPS)
            slots_io(2)
            slots_io(3)
            for q in range(GROUPS):
                tiles = slice(q * GT, (q + 1) * GT)
                sp.wait_ge(combined, TOP * GT * (GROUPS + q + 1))
                sp.dma_start(out_tiles[:, tiles, :], xs[:, tiles, :]).then_inc(out_stored, 16)
            sp.wait_ge(out_stored, 16 * GROUPS)

        @block.gpsimd
        def _(pool):
            pool.memset(zeros, 0.0).then_inc(zeros_ready, 1)
            pool.memset(ident[:, :], 0.0)
            pool.memset(ident_bf[:, :], 0.0)
            pool.memset(causal_bf[:, :], 0.0)
            pool.memset(before_bf[:, :], 1.0)
            pool.memset(ones_bf[:, :], 1.0)
            pool.memset(upto[:, :, :], 1.0).then_inc(const_ready, 1)
            pool.wait_ge(const_ready, 1)
            for m in (ident, ident_bf):
                pool.affine_select(out=m[:, :], in_=m[:, :], compare_op=ALU.not_equal, fill=1.0, base=0,
                                   pattern=[[-1, P]], channel_multiplier=1)
            pool.affine_select(out=causal_bf[:, :], in_=causal_bf[:, :], compare_op=ALU.is_ge, fill=MASKED, base=0,
                               pattern=[[-1, P]], channel_multiplier=1)
            pool.affine_select(out=before_bf[:, :], in_=before_bf[:, :], compare_op=ALU.is_gt, fill=0.0, base=0,
                               pattern=[[1, P]], channel_multiplier=-1)
            pool.affine_select(out=upto[:, :, :], in_=upto[:, :, :], compare_op=ALU.is_ge, fill=0.0, base=0,
                               pattern=[[1, EXPERTS], [-1, EXPERTS]], channel_multiplier=0)
            pool.iota(rank[:, :], pattern=[[-1, EXPERTS]], base=EXPERTS, channel_multiplier=0,
                      allow_small_or_imprecise_dtypes=True)
            pool.iota(tile_start[:, :], pattern=[[P, GT]], base=0, channel_multiplier=0,
                      allow_small_or_imprecise_dtypes=True)
            pool.iota(tile_no[:, :], pattern=[[1, SLOT_TILES]], base=0, channel_multiplier=0,
                      allow_small_or_imprecise_dtypes=True).then_inc(const_ready, 1)

            def scatter(f):
                q = f % GROUPS
                pool.wait_ge(routed, f + 1)
                for k in range(TOP):
                    for t in range(GT):
                        pool.indirect_dma_start(
                            out=x_slots[q][:, :], out_offset=bass.IndirectOffsetOnAxis(ap=slot[q][:, k, t:t + 1], axis=0),
                            in_=xn_all[q][:, t, :], in_offset=None).then_inc(scattered[f], 16)

            def gather(f):
                q = f % GROUPS
                for par in range(2):
                    pool.wait_ge(y_stored[f][par], 16 * SLOT_TILES // 2)
                for t in range(GT):
                    for k in range(TOP):
                        j, ring = TOP * t + k, (TOP * t + k) % ring_of(f)
                        wait(pool, combined, f * TOP * GT + j - ring_of(f) + 1)
                        pool.indirect_dma_start(
                            out=yg[ring], out_offset=None, in_=y_slots[q][:, :],
                            in_offset=bass.IndirectOffsetOnAxis(ap=slot[q][:, k, t:t + 1], axis=0),
                        ).then_inc(gathered[f][ring], 16)

            for q in range(GROUPS):
                pool.wait_ge(zeroed[q], 16 * ZERO_FILLS)
                scatter(q)
            gather(0)
            gather(1)
            scatter(2)
            scatter(3)
            gather(2)
            gather(3)

        @block.scalar
        def _(act):
            act.dma_start(wr_sb[:, :], w_r).then_inc(router_w_loaded, 16)
            act.dma_start(br_bc[:, :], b_r.rearrange("(o e) -> o e", o=1).broadcast_to([P, EXPERTS])).then_inc(router_w_loaded, 16)
            act.dma_start(b1_nat, b_1.rearrange("e (c p) -> (e c) p", p=P)).then_inc(w_loaded, 16)
            act.dma_start(w1_raw[:, :].rearrange("d (e n) -> d e n", e=EXPERTS), w_1.rearrange("e d n -> d e n")).then_inc(ffn_w_loaded, 16)
            act.wait_ge(zeros_ready, 1)
            for q in range(GROUPS):
                for n in range(ZERO_FILLS):
                    rows = x_slots[q][n * 8 * P:(n + 1) * 8 * P, :].rearrange("(p r) d -> p (r d)", p=P)
                    act.dma_start(rows, zeros).then_inc(zeroed[q], 16)
            act.dma_start(w2_sb[:, :].rearrange("p (e d) -> p e d", d=D), w_2.rearrange("e (c p) d -> p (e c) d", p=P)).then_inc(w2_loaded, 16)
            act.dma_start(b2_bc[:, :, :], b_2.rearrange("(o e) d -> o e d", o=1).broadcast_to([P, EXPERTS, D])).then_inc(w2_loaded, 16)

            def split_w1():
                act.wait_ge(ffn_w_loaded, 16)
                for n in range(4):
                    cols = slice(n * 1024, (n + 1) * 1024)
                    act.activation(w1_hi[:, cols], w1_raw[:, cols], ACT.Copy).then_inc(w1_hi_ready, 1)

            def take_for_router(f, l):
                for g in range(GB):
                    act.wait_ge(tr_ps, GB * l + g + 1)
                    wait(act, logits_ps, GB * f + g - 1)
                    act.activation(xt_r[g % 2], bank[6 + g % 2][:, :], ACT.Copy).then_inc(tr_taken, 1)

            def take_gates(f):
                act.wait_ge(delta_ready, f + 1)
                act.activation(top[3][:, :], top[2][:, :], ACT.Exp).then_inc(exp_delta, 1)

            def take_for_attention(l):
                for g in range(GB):
                    act.wait_ge(tr_ps, GB * l + g + 1)
                    cols = slice(g * SEQ, (g + 1) * SEQ)
                    act.activation(xn_hi[:, cols], bank[6 + g % 2][:, :], ACT.Copy)
                    act.activation(xn_t[:, cols], bank[6 + g % 2][:, :], ACT.Copy).then_inc(xnt_done, 1)

            def prepare_weights():
                for n in range(HEADS // 4):
                    act.wait_ge(kq_ps, n + 1)
                    act.activation(kq[:, 4 * n:4 * n + 4, 0, :], bank[n % 2][:, :].rearrange("p (a e) -> p a e", a=4),
                                   ACT.Copy, scale=SCALE).then_inc(kq_hi_ready, 1)
                for n, dst in enumerate((wv_t[:, 0:512], wv_t[:, 512:1024], wo_t[:, 0:512], wo_t[:, 512:1024])):
                    act.wait_ge(wt_ps, n + 1)
                    act.activation(dst, bank[2 + n % 2][:, :], ACT.Copy).then_inc(wt_ready, 1)
                act.wait_ge(wt_ps, 5)
                act.activation(b1_t[:, :], bank[4][:, 0:EXPERTS * CHUNKS], ACT.Copy).then_inc(wt_ready, 1)

            def experts(f):
                q = f % GROUPS
                act.wait_ge(routed, f + 1)

                def high(n, u):
                    c = f * SLOT_TILES + n
                    act.wait_ge(xgt_ps, c + 1)
                    wait(act, up_ps, c - 1)
                    act.activation(xg_hi[u % 2][:, :], bank[u % 2][:, 0:P], ACT.Copy).then_inc(xg_hi_ready, 1)

                def relu(n, u, e):
                    c = f * SLOT_TILES + n
                    act.wait_ge(ht_ps, c + 1)
                    wait(act, y_ps, c - 1)
                    for k in range(CHUNKS):
                        ins = act.activation(h_t[u % 2][:, k, :], bank[4 + u % 2][:, k * P:(k + 1) * P], ACT.Relu,
                                             bias=b1_t[:, bass.ds(e * CHUNKS + k, 1)])
                    ins.then_inc(ht_ready, 1)

                high(0, 0)

                def turn(m):
                    first = isinstance(m, int) and m == 0
                    e = experts_of(mybir.EngineType.Activation, q, 0 if first else UNROLL * m - 1,
                                   UNROLL if first else UNROLL + 1)
                    e = [None, *e] if first else e
                    for u in range(UNROLL):
                        n = UNROLL * m + u
                        if not (isinstance(m, int) and n + 1 >= SLOT_TILES):
                            high(n + 1, u + 1)
                        if not (isinstance(m, int) and n == 0):
                            relu(n - 1, u + 3, e[u])
                    if isinstance(m, int) and m > 0:
                        relu(SLOT_TILES - 1, 3, e[UNROLL])

                slot_tiles(act, turn)

            def take_g(i, par, h):
                act.wait_ge(g_ps, 2 * i + h + 1)
                wait(act, s_ps, S_USES * (2 * (i - 2) + h + 1))
                act.activation(g_hi[par][:, h, :], J_BANK[(3 * par + h) % 2][:, :], ACT.Copy).then_inc(g_hi_ready, 1)

            def take_v(i, par):
                act.wait_ge(v_ps, i + 1)
                wait(act, z_ps, i - 1)
                act.activation(v_sb[par][:, :, :], J_BANK[(3 * par + 2) % 2][:, :].rearrange("p (k m) -> p k m", m=P),
                               ACT.Copy).then_inc(v_ready, 1)

            def exps(i, h, tiles):
                head = 2 * i + h
                for t in tiles:
                    act.wait_ge(max_ready, QT * head + max(t + 1, 2))
                    if t == 0:
                        wait(act, pt_ps, 3 * (head - 1))
                        wait(act, inv_ready, head - 1)
                    act.activation(probs[h][:, t, 0:(t + 1) * P], score_tile(t, slice(0, (t + 1) * P)), ACT.Exp,
                                   bias=neg_max[:, h, t:t + 1], accum_out=row_sum[:, h, t:t + 1]).then_inc(exp_done, 1)

            def transposed(i, h):
                head = 2 * i + h
                act.wait_ge(pt_ps, 3 * head + 1)
                wait(act, z_ps, i)
                act.activation(probs_t[h][:, 0, :], T_BANK[h % 2][:, :], ACT.Copy).then_inc(pt_act, 1)

            def attention(half):
                start = half * STEPS // GROUPS
                take_g(start, 0, 0)
                take_g(start, 0, 1)
                take_v(start, 0)

                def step(i, par, first, last):
                    if not first:
                        transposed(i - 1, 1)
                    exps(i, 0, [0, 1, 2, 3])
                    if not last:
                        take_g(i + 1, 1 - par, 0)
                        take_g(i + 1, 1 - par, 1)
                    transposed(i, 0)
                    exps(i, 1, [0, 1, 2, 3])
                    if not last:
                        take_v(i + 1, 1 - par)
                    else:
                        transposed(i, 1)

                attention_steps(act, half, step)

            take_for_router(0, 0)
            split_w1()
            take_gates(0)
            prepare_weights()
            take_for_router(1, 1)
            take_gates(1)
            experts(0)
            experts(1)
            take_for_attention(2)
            attention(0)
            take_for_attention(3)
            take_for_router(2, 4)
            take_gates(2)
            attention(1)
            take_for_router(3, 5)
            take_gates(3)
            experts(2)
            experts(3)

        @block.vector
        def _(dve):
            chained = [0]

            def link(ins):
                chained[0] += 1
                ins.then_inc(chain, 1)
                dve.wait_ge(chain, chained[0])

            def split_w1():
                for n in range(4):
                    cols = slice(n * 1024, (n + 1) * 1024)
                    dve.wait_ge(w1_hi_ready, n + 1)
                    dve.tensor_tensor(w1_lo[:, cols], w1_raw[:, cols], w1_hi[:, cols].bitcast(fp32),
                                      ALU.subtract).then_inc(w1_lo_ready, 1)

            def split_kq():
                for n in range(HEADS // 4):
                    dve.wait_ge(kq_hi_ready, n + 1)
                    dve.scalar_tensor_tensor(
                        out=kq[:, 4 * n:4 * n + 4, 1, :], in0=bank[n % 2][:, :].rearrange("p (a e) -> p a e", a=4),
                        scalar=SCALE, in1=kq[:, 4 * n:4 * n + 4, 0, :].bitcast(fp32), op0=ALU.mult, op1=ALU.subtract,
                    ).then_inc(kq_lo_ready, 1)

            def layer_norm(q, l, buffer, split=False):
                def stats(b):
                    for t in range(QT):
                        ins = dve.bn_stats(bn[:, bass.ds(b * QT + t, 1), :].rearrange("p o d -> p (o d)"),
                                           tile_of(q * GB + b, t))
                    return ins

                stats(0)
                with dve.Fori(1, GB - 1) as b:
                    stats(b)
                link(stats(GB - 1))
                dve.tensor_tensor(mean[:, :], bn[:, :, 1], bn[:, :, 4], ALU.add)
                dve.tensor_tensor(half_var[:, :], bn[:, :, 2], bn[:, :, 5], ALU.add)
                link(dve.tensor_tensor(ln_t[:, :], bn[:, :, 1], bn[:, :, 4], ALU.subtract))
                link(dve.tensor_tensor(ln_t[:, :], ln_t[:, :], ln_t[:, :], ALU.mult))
                dve.tensor_scalar(mean[:, :], mean[:, :], 0.5, None, ALU.mult)
                link(dve.tensor_scalar(half_var[:, :], half_var[:, :], -0.5 / D, -0.5 * EPS, ALU.mult, ALU.add))
                link(dve.scalar_tensor_tensor(out=half_var[:, :], in0=ln_t[:, :], scalar=-0.125, in1=half_var[:, :],
                                              op0=ALU.mult, op1=ALU.add))
                link(dve.tensor_scalar(ln_t[:, :], half_var[:, :], -2.0, None, ALU.mult))
                link(dve.tensor_scalar(rstd[:, :].bitcast(mybir.dt.int32), ln_t[:, :].bitcast(mybir.dt.int32), 1, None,
                                       ALU.logical_shift_right))
                link(dve.tensor_scalar(rstd[:, :].bitcast(mybir.dt.int32), rstd[:, :].bitcast(mybir.dt.int32), -1.0,
                                       float(0x5F3759DF), ALU.mult, ALU.add))
                for _ in range(3):
                    link(dve.tensor_tensor(ln_t[:, :], rstd[:, :], rstd[:, :], ALU.mult))
                    link(dve.tensor_tensor(ln_t[:, :], ln_t[:, :], half_var[:, :], ALU.mult))
                    link(dve.scalar_tensor_tensor(out=rstd[:, :], in0=ln_t[:, :], scalar=1.5, in1=rstd[:, :],
                                                  op0=ALU.add, op1=ALU.mult))

                def normalise_block(b):
                    for t in range(QT):
                        i = bass.ds(b * QT + t, 1)
                        ins = dve.tensor_scalar(xn_all[buffer][:, i, :].rearrange("p o d -> p (o d)"),
                                                tile_of(q * GB + b, t), mean[:, i], rstd[:, i], ALU.subtract, ALU.mult)
                    ins.then_inc(xn_ready, 1)

                def split_block(g):
                    cols = slice(g * SEQ, (g + 1) * SEQ)
                    dve.wait_ge(xnt_done, GB * (l - 2) + g + 1)
                    dve.tensor_tensor(xn_lo[:, cols], bank[6 + g % 2][:, :], xn_hi[:, cols].bitcast(fp32),
                                      ALU.subtract).then_inc(tr_taken, 1)

                for b in range(GB):
                    normalise_block(b)
                    if split and b > 0:
                        split_block(b - 1)
                if split:
                    split_block(GB - 1)

            def route(f):
                q = f % GROUPS
                logit, a, b, hot1, hot2, place = rt
                m1, k1, delta, e_delta = top
                over_e = [P, GT, EXPERTS]

                def wide(per_token):
                    return per_token.rearrange("p (t o) -> p t o", o=1).broadcast_to(over_e)

                def per_expert(row):
                    return row.rearrange("p (o e) -> p o e", o=1).broadcast_to(over_e)

                dve.wait_ge(logits_ps, GB * (f + 1))
                link(dve.tensor_tensor(logit, bank[5][:, 0:GT * EXPERTS].rearrange("p (t e) -> p t e", e=EXPERTS),
                                       per_expert(br_bc[:, :]), ALU.add))

                def hottest(values, largest, hot):
                    link(dve.tensor_reduce(largest, values, AX.X, ALU.max))
                    link(dve.tensor_tensor(b, values, wide(largest), ALU.is_equal))
                    link(dve.tensor_tensor(b, b, per_expert(rank[:, :]), ALU.mult))
                    link(dve.tensor_reduce(k1[:, :], b, AX.X, ALU.max))
                    link(dve.tensor_tensor(hot, per_expert(rank[:, :]), wide(k1[:, :]), ALU.is_equal))

                hottest(logit, m1[:, :], hot1)
                link(dve.scalar_tensor_tensor(out=a, in0=hot1, scalar=-3e38, in1=logit, op0=ALU.mult, op1=ALU.add))
                hottest(a, delta[:, :], hot2)
                dve.tensor_tensor(count_bf[:, :].rearrange("p (t e) -> p t e", e=EXPERTS), hot1, hot2,
                                  ALU.add).then_inc(counts_ready, 1)
                dve.tensor_tensor(delta[:, :], delta[:, :], m1[:, :], ALU.subtract).then_inc(delta_ready, 1)
                dve.wait_ge(exp_delta, f + 1)
                link(dve.tensor_scalar(k1[:, :], e_delta[:, :], 1.0, 2.0, ALU.add, ALU.mult))
                link(dve.reciprocal(gate[q][:, :, 0], k1[:, :]))
                dve.tensor_tensor(gate[q][:, :, 1], gate[q][:, :, 0], e_delta[:, :], ALU.mult)

                dve.wait_ge(places_ps, f + 1)
                placed = bank[5][:, 0:GT * EXPERTS].rearrange("p (t e) -> p t e", e=EXPERTS)
                number, tiles, ends, base = (ex[:, i, :] for i in range(4))
                link(dve.tensor_copy(number, bank[5][:, GT * EXPERTS:(GT + 1) * EXPERTS]))
                over = rt2[0][:, 0:EXPERTS * GT].rearrange("p (e j) -> p e j", j=GT)
                link(dve.tensor_tensor(over, number.rearrange("p (e o) -> p e o", o=1).broadcast_to([P, EXPERTS, GT]),
                                       tile_start[:, :].rearrange("p (o j) -> p o j", o=1).broadcast_to([P, EXPERTS, GT]),
                                       ALU.is_gt))
                link(dve.tensor_reduce(tiles, over, AX.X, ALU.add))
                sums = rt2[0][:, 0:EXPERTS * EXPERTS].rearrange("p (e g) -> p e g", g=EXPERTS)
                link(dve.tensor_tensor(sums, upto[:, :, :],
                                       tiles.rearrange("p (o g) -> p o g", o=1).broadcast_to([P, EXPERTS, EXPERTS]),
                                       ALU.mult))
                link(dve.tensor_reduce(ends, sums, AX.X, ALU.add))
                link(dve.tensor_tensor(base, ends, tiles, ALU.subtract))
                link(dve.tensor_scalar(base, base, float(P), None, ALU.mult))
                link(dve.tensor_tensor(place, placed, per_expert(base), ALU.add))
                for k, hot in enumerate((hot1, hot2)):
                    link(dve.tensor_tensor(a, place, hot, ALU.mult))
                    link(dve.tensor_reduce(k1[:, :], a, AX.X, ALU.add))
                    link(dve.tensor_copy(slot[q][:, k, :], k1[:, :]))
                ended = rt2[1][:, :].rearrange("p (n e) -> p n e", e=EXPERTS)
                link(dve.tensor_tensor(ended, tile_no[:, :].rearrange("p (n o) -> p n o", o=1).broadcast_to([P, SLOT_TILES, EXPERTS]),
                                       ends.rearrange("p (o e) -> p o e", o=1).broadcast_to([P, SLOT_TILES, EXPERTS]),
                                       ALU.is_ge))
                link(dve.tensor_reduce(rt2[0][:, 0:SLOT_TILES], ended, AX.X, ALU.add))
                dve.tensor_scalar(expert_of[q][:, :], rt2[0][:, 0:SLOT_TILES], float(EXPERTS - 1), None,
                                  ALU.min).then_inc(routed, 1)

            def experts(f, combining=None):
                q = f % GROUPS

                def low(n, u):
                    c = f * SLOT_TILES + n
                    dve.wait_ge(xg_hi_ready, c + 1)
                    wait(dve, up_ps, c - 1)
                    dve.tensor_tensor(xg_lo[u % 2][:, :], bank[u % 2][:, 0:P], xg_hi[u % 2][:, :].bitcast(fp32),
                                      ALU.subtract).then_inc(xg_lo_ready, 1)

                def take_up(n, u):
                    c = f * SLOT_TILES + n
                    dve.wait_ge(up_ps, c + 1)
                    wait(dve, ht_ps, c - 1)
                    dve.tensor_copy(h_sb[u % 2], bank[2 + u % 2][:, :]).then_inc(up_ready, 1)

                def take_y(n, u, e):
                    c = f * SLOT_TILES + n
                    dve.wait_ge(y_ps, c + 1)
                    wait(dve, y_stored[f][u % 2], 16 * (n // 2))
                    dve.tensor_tensor(y_sb[u % 2], bank[6 + u % 2][:, 0:P],
                                      b2_bc[:, bass.ds(e, 1), :].rearrange("p o d -> p (o d)"), ALU.add).then_inc(y_ready, 1)

                dve.wait_ge(routed, f + 1)
                if f > 0:
                    for par in range(2):
                        dve.wait_ge(y_stored[f - 1][par], 16 * SLOT_TILES // 2)
                low(0, 0)

                def turn(m):
                    first = isinstance(m, int) and m == 0
                    e = experts_of(mybir.EngineType.DVE, q, 0 if first else UNROLL * m - 2,
                                   UNROLL if first else UNROLL + 2)
                    e = [None, None, *e] if first else e
                    for u in range(UNROLL):
                        n = UNROLL * m + u
                        if not (isinstance(m, int) and n + 1 >= SLOT_TILES):
                            low(n + 1, u + 1)
                        take_up(n, u)
                        if not (isinstance(m, int) and n < 2):
                            take_y(n - 2, u + 2, e[u])
                        if combining is not None and not isinstance(m, int):
                            combine(combining, (m - 1) * (UNROLL // TOP) + u // TOP, u % TOP, u, m)
                    if isinstance(m, int) and m > 0:
                        take_y(SLOT_TILES - 2, 2, e[UNROLL])
                        take_y(SLOT_TILES - 1, 3, e[UNROLL + 1])

                slot_tiles(dve, turn)

            def combine(f, t, k, ring, use):
                q = f % GROUPS
                dve.wait_ge(gathered[f][ring], 16 * use)
                if k > 0:
                    dve.wait_ge(combined, f * TOP * GT + TOP * t + k)
                tokens = tile_of(q * GB, t)
                dve.scalar_tensor_tensor(
                    out=tokens, in0=yg[ring], scalar=gate[q][:, bass.ds(t, 1), k], in1=tokens,
                    op0=ALU.mult, op1=ALU.add).then_inc(combined, 1)

            def combine_all(f):
                def tiles(b):
                    for s in range(RING):
                        combine(f, b * (RING // TOP) + s // TOP, s % TOP, s, b + 1)

                tiles(0)
                with dve.Fori(1, TOP * GT // RING) as b:
                    tiles(b)

            def take_g(i, par, h):
                dve.wait_ge(g_hi_ready, 2 * i + h + 1)
                wait(dve, s_ps, S_USES * (2 * (i - 2) + h + 1))
                dve.tensor_tensor(g_lo[par][:, h, :], J_BANK[(3 * par + h) % 2][:, :],
                                  g_hi[par][:, h, :].bitcast(fp32), ALU.subtract).then_inc(g_lo_ready, 1)

            def maxima(i, h):
                head = 2 * i + h
                for t in range(QT):
                    dve.wait_ge(s_ps, S_USES * head + S_USE[t] + 1)
                    if t == 0:
                        wait(dve, exp_done, QT * (head - 1))
                    dve.tensor_reduce(neg_max[:, h, t:t + 1], score_tile(t, slice(0, (t + 1) * P)), AX.X, ALU.max,
                                      negate=True).then_inc(max_ready, 1)

            def invert(i, h, par):
                head = 2 * i + h
                dve.wait_ge(exp_done, QT * (head + 1))
                wait(dve, inv_stored, 16 * (i - 1))
                if h == 1:
                    wait(dve, z_ready, i - 1)
                dve.reciprocal(inv_sum[par][:, h, :], row_sum[:, h, :]).then_inc(inv_ready, 1)

            def transposed(i, h, use):
                head = 2 * i + h
                dve.wait_ge(pt_ps, 3 * head + use + 1)
                wait(dve, z_ps, i)
                src = T_BANK[(h + use) % 2]
                if use == 1:
                    dve.tensor_copy(probs_t[h][:, 1, P:SEQ], src[:, 0:3 * P]).then_inc(pt_dve, 1)
                else:
                    dve.tensor_copy(probs_t[h][:, 2, 2 * P:SEQ], src[:, 0:2 * P])
                    dve.tensor_copy(probs_t[h][:, 3, 3 * P:SEQ], src[:, 2 * P:3 * P]).then_inc(pt_dve, 1)

            def normalise(i, par):
                dve.wait_ge(z_ps, i + 1)
                dve.wait_ge(inv_loaded[par], 32 * (i // 2 + 1))
                wait(dve, o_ps, i)
                dve.tensor_tensor(z_sb[:, :].rearrange("p (t q) -> p t q", t=QT),
                                  ZO_BANK[:, :].rearrange("p (t q) -> p t q", t=QT),
                                  inv_bc[par][:, :, :].rearrange("p q t -> p t q"), ALU.mult).then_inc(z_ready, 1)

            def add_out(i, half):
                dve.wait_ge(o_ps, i + 1)
                wait(dve, o_added, i)
                tokens = xs[:, bass.ds((i // PAIRS) * QT, QT), :]
                dve.tensor_tensor(tokens, ZO_BANK[:, :].rearrange("p (t d) -> p t d", t=QT), tokens,
                                  ALU.add).then_inc(o_added, 1)

            def attention(half, combining=None):
                start = half * STEPS // GROUPS
                take_g(start, 0, 0)
                take_g(start, 0, 1)

                def step(i, par, first, last):
                    maxima(i, 0)
                    if not first:
                        transposed(i - 1, 1, 1)
                    if combining is not None:
                        combine(combining, i // TOP, par, par, i // TOP + 1)
                    if not first:
                        transposed(i - 1, 1, 2)
                    if not last:
                        take_g(i + 1, 1 - par, 0)
                        take_g(i + 1, 1 - par, 1)
                    invert(i, 0, par)
                    if not first:
                        normalise(i - 1, 1 - par)
                    maxima(i, 1)
                    transposed(i, 0, 1)
                    transposed(i, 0, 2)
                    invert(i, 1, par)
                    if not first:
                        add_out(i - 1, half)
                    if last:
                        transposed(i, 1, 1)
                        transposed(i, 1, 2)
                        normalise(i, par)
                        add_out(i, half)

                attention_steps(dve, half, step)

            dve.wait_ge(x_loaded[0], 16)
            layer_norm(0, 0, 0)
            dve.wait_ge(router_w_loaded, 32)
            dve.wait_ge(const_ready, 2)
            route(0)
            split_w1()
            split_kq()
            dve.wait_ge(w1_lo_ready, 4)
            dve.wait_ge(x_loaded[1], 16)
            layer_norm(1, 1, 1)
            route(1)
            dve.wait_ge(w2_loaded, 32)
            experts(0)
            experts(1, combining=0)
            dve.wait_ge(scattered[1], 16 * TOP * GT)
            dve.wait_ge(combined, TOP * GT)
            layer_norm(0, 2, 1, split=True)
            attention(0, combining=1)
            dve.wait_ge(combined, TOP * GT * 2)
            layer_norm(1, 3, 1, split=True)
            dve.wait_ge(o_added, STEPS // 2)
            layer_norm(0, 4, 0)
            route(2)
            attention(1)
            dve.wait_ge(o_added, STEPS)
            layer_norm(1, 5, 1)
            route(3)
            experts(2)
            experts(3, combining=2)
            combine_all(3)

        @block.tensor
        def _(pe):
            def transpose_tokens(l, buffer):
                for g in range(GB):
                    pe.wait_ge(xn_ready, GB * l + g + 1)
                    wait(pe, tr_taken, GB * l + g - 1)
                    for t in range(QT):
                        ins = pe.transpose(bank[6 + g % 2][:, t * P:(t + 1) * P], xn_all[buffer][:, g * QT + t, :],
                                           ident[:, :])
                    ins.then_inc(tr_ps, 1)
                    yield g

            def route(f, l):
                q = f % GROUPS

                def logits(g):
                    pe.wait_ge(tr_taken, GB * l + g + 1)
                    for t in range(QT):
                        at = (g * QT + t) * EXPERTS
                        ins = pe.matmul(bank[5][:, at:at + EXPERTS], xt_r[g % 2][:, t * P:(t + 1) * P], wr_sb[:, :],
                                        start=True, stop=True)
                    ins.then_inc(logits_ps, 1)

                for g in transpose_tokens(l, q):
                    if g > 0:
                        logits(g - 1)
                logits(GB - 1)
                pe.wait_ge(counts_ready, f + 1)
                width = GT * EXPERTS
                pe.matmul(bank[5][:, 0:width], before_bf[:, :], count_bf[:, :], start=True, stop=False)
                for t in range(1, GT):
                    pe.matmul(bank[5][:, t * EXPERTS:width], ones_bf[:, :], count_bf[:, 0:width - t * EXPERTS],
                              start=False, stop=(t == GT - 1))
                for t in range(GT):
                    ins = pe.matmul(bank[5][:, width:width + EXPERTS], ones_bf[:, :],
                                    count_bf[:, t * EXPERTS:(t + 1) * EXPERTS], start=(t == 0), stop=(t == GT - 1))
                ins.then_inc(places_ps, 1)

            def prepare_weights():
                pe.wait_ge(w_loaded, 80)
                for n in range(HEADS // 4):
                    wait(pe, kq_lo_ready, n - 1)
                    for a in range(4):
                        ins = pe.matmul(bank[n % 2][:, a * D:(a + 1) * D], wk_nat[:, 4 * n + a, :],
                                        wq_nat[:, 4 * n + a, :], start=True, stop=True)
                    ins.then_inc(kq_ps, 1)
                for n in range(4):
                    wait(pe, wt_ready, n - 1)
                    for a in range(4):
                        j = 4 * (n % 2) + a
                        src = wv_nat[:, j, :] if n < 2 else wo_nat[:, 2 * j:2 * j + 2, :].rearrange("e a h -> e (a h)")
                        ins = pe.transpose(bank[2 + n % 2][:, a * P:(a + 1) * P], src, ident[:, :])
                    ins.then_inc(wt_ps, 1)
                rows = EXPERTS * CHUNKS
                pe.transpose(bank[4][:, 0:rows], b1_nat, ident[0:rows, 0:rows]).then_inc(wt_ps, 1)

            def experts(f):
                q = f % GROUPS
                pe.wait_ge(routed, f + 1)
                pe.wait_ge(tr_taken, GB * (2 if f < GROUPS else 6))

                def transpose_x(n, u):
                    c = f * SLOT_TILES + n
                    pe.wait_ge(xg_loaded[u % 4], 16 * (f * SLOT_TILES // 4 + n // 4 + 1))
                    wait(pe, xg_lo_ready, c - 1)
                    pe.transpose(bank[u % 2][:, 0:P], xg[u % 4], ident[:, :]).then_inc(xgt_ps, 1)

                def up(n, u, e):
                    c = f * SLOT_TILES + n
                    cols = bass.ds(e * HIDDEN, HIDDEN)
                    pe.wait_ge(xg_lo_ready, c + 1)
                    wait(pe, up_ready, c - 1)
                    dst = bank[2 + u % 2][:, :]
                    pe.matmul(dst, xg_lo[u % 2][:, :], w1_hi[:, cols], start=True, stop=False)
                    pe.matmul(dst, xg_hi[u % 2][:, :], w1_lo[:, cols], start=False, stop=False)
                    pe.matmul(dst, xg_hi[u % 2][:, :], w1_hi[:, cols], start=False, stop=True).then_inc(up_ps, 1)

                def transpose_h(n, u):
                    c = f * SLOT_TILES + n
                    pe.wait_ge(up_ready, c + 1)
                    wait(pe, ht_ready, c - 1)
                    for k in range(CHUNKS):
                        ins = pe.transpose(bank[4 + u % 2][:, k * P:(k + 1) * P], h_sb[u % 2][:, k * P:(k + 1) * P],
                                           ident[:, :])
                    ins.then_inc(ht_ps, 1)

                def down(n, u, e):
                    c = f * SLOT_TILES + n
                    pe.wait_ge(ht_ready, c + 1)
                    wait(pe, y_ready, c - 1)
                    for k in range(CHUNKS):
                        ins = pe.matmul(bank[6 + u % 2][:, 0:P], h_t[u % 2][:, k, :],
                                        w2_sb[:, bass.ds(e * (CHUNKS * D) + k * D, D)],
                                        start=(k == 0), stop=(k == CHUNKS - 1))
                    ins.then_inc(y_ps, 1)

                transpose_x(0, 0)

                def turn(m):
                    first = isinstance(m, int) and m == 0
                    e = experts_of(mybir.EngineType.PE, q, 0 if first else UNROLL * m - 2,
                                   UNROLL if first else UNROLL + 2)
                    e = [None, None, *e] if first else e
                    for u in range(UNROLL):
                        n = UNROLL * m + u
                        if not (isinstance(m, int) and n + 1 >= SLOT_TILES):
                            transpose_x(n + 1, u + 1)
                        up(n, u, e[u + 2])
                        if not (isinstance(m, int) and n < 1):
                            transpose_h(n - 1, u + 3)
                        if not (isinstance(m, int) and n < 2):
                            down(n - 2, u + 2, e[u])
                    if isinstance(m, int) and m > 0:
                        transpose_h(SLOT_TILES - 1, 3)
                        down(SLOT_TILES - 2, 2, e[UNROLL])
                        down(SLOT_TILES - 1, 3, e[UNROLL + 1])

                slot_tiles(pe, turn)

            def project_g(i, par, h, half):
                cols = bass.ds(seq_of(i, half) * SEQ, SEQ)
                if h == 0:
                    pe.wait_ge(staged[par], 32 * (i // 2 + 1))
                    wait(pe, g_lo_ready, 2 * i)
                else:
                    wait(pe, v_ready, i)
                dst = J_BANK[(3 * par + h) % 2][:, :]
                pe.matmul(dst, kq_st[par][:, h, 1, :], xn_hi[:, cols], start=True, stop=False)
                pe.matmul(dst, kq_st[par][:, h, 0, :], xn_lo[:, cols], start=False, stop=False)
                pe.matmul(dst, kq_st[par][:, h, 0, :], xn_hi[:, cols], start=False, stop=True).then_inc(g_ps, 1)

            def project_v(i, par):
                pe.wait_ge(g_lo_ready, 2 * i + 1)
                dst = J_BANK[(3 * par + 2) % 2]
                for k in range(QT):
                    ins = pe.matmul(dst[:, k * P:(k + 1) * P], xn_st[par][:, k * P:(k + 1) * P],
                                    wv_t[:, bass.ds(pair_of(i) * P, P)], start=True, stop=True)
                ins.then_inc(v_ps, 1)

            def scores(i, h, par, tiles, half):
                head = 2 * i + h
                for t in tiles:
                    if t == 0:
                        pe.wait_ge(g_lo_ready, head + 1)
                    if t != 1:
                        wait(pe, exp_done, QT * (head - 1) + max(t + 1, 2))
                    cols = bass.ds(seq_of(i, half) * SEQ, keys_of[t])
                    q = slice(t * P, (t + 1) * P)
                    dst = score_tile(t, slice(0, keys_of[t]))
                    pe.matmul(dst, g_lo[par][:, h, q], xn_hi[:, cols], start=True, stop=False)
                    pe.matmul(dst, g_hi[par][:, h, q], xn_lo[:, cols], start=False, stop=False)
                    pe.matmul(dst, g_hi[par][:, h, q], xn_hi[:, cols], start=False, stop=False)
                    ins = pe.matmul(score_tile(t, q), ident_bf[:, :], causal_bf[:, :], start=False, stop=True)
                    if t > 0:
                        ins.then_inc(s_ps, 1)

            def transposes(i, h, use):
                head = 2 * i + h
                src = probs[h]
                dst = T_BANK[(h + use) % 2]
                if use == 0:
                    pe.wait_ge(exp_done, QT * (head + 1))
                    wait(pe, pt_dve, 2 * head - 1)
                    for t in range(QT):
                        ins = pe.transpose(dst[:, t * P:(t + 1) * P], src[:, t, 0:P], ident[:, :])
                if use == 1:
                    wait(pe, pt_dve, 2 * head)
                    for t in range(1, QT):
                        ins = pe.transpose(dst[:, (t - 1) * P:t * P], src[:, t, P:2 * P], ident[:, :])
                if use == 2:
                    pe.wait_ge(pt_act, head + 1)
                    pe.transpose(dst[:, 0:P], src[:, 2, 2 * P:3 * P], ident[:, :])
                    pe.transpose(dst[:, P:2 * P], src[:, 3, 2 * P:3 * P], ident[:, :])
                    ins = pe.transpose(dst[:, 2 * P:3 * P], src[:, 3, 3 * P:4 * P], ident[:, :])
                ins.then_inc(pt_ps, 1)

            def attend(i, par):
                pe.wait_ge(v_ready, i + 1)
                pe.wait_ge(pt_act, 2 * i + 2)
                wait(pe, o_added, i)
                for k in range(QT):
                    if k in (1, 2):
                        pe.wait_ge(pt_dve, 4 * i + 2 + k)
                    for h in range(2):
                        m = slice(h * DH, (h + 1) * DH)
                        ins = pe.matmul(ZO_BANK[m, k * P:SEQ], v_sb[par][:, k, m], probs_t[h][:, k, k * P:SEQ],
                                        start=(k == 0), stop=(k == QT - 1))
                ins.then_inc(z_ps, 1)

            def project_out(i):
                pe.wait_ge(z_ready, i + 1)
                for t in range(QT):
                    ins = pe.matmul(ZO_BANK[:, t * D:(t + 1) * D], z_sb[:, t * P:(t + 1) * P],
                                    wo_t[:, bass.ds(pair_of(i) * D, D)], start=True, stop=True)
                ins.then_inc(o_ps, 1)

            def attention(half):
                start = half * STEPS // GROUPS
                project_g(start, 0, 0, half)
                project_g(start, 0, 1, half)
                project_v(start, 0)

                def step(i, par, first, last):
                    scores(i, 0, par, [0, 1, 2], half)
                    if not first:
                        transposes(i - 1, 1, 0)
                    scores(i, 0, par, [3], half)
                    if not first:
                        transposes(i - 1, 1, 1)
                    if not last:
                        project_g(i + 1, 1 - par, 0, half)
                    if not first:
                        transposes(i - 1, 1, 2)
                    if not last:
                        project_g(i + 1, 1 - par, 1, half)
                    if not first:
                        attend(i - 1, 1 - par)
                    scores(i, 1, par, [0, 1, 2], half)
                    transposes(i, 0, 0)
                    scores(i, 1, par, [3], half)
                    transposes(i, 0, 1)
                    if not last:
                        project_v(i + 1, 1 - par)
                    transposes(i, 0, 2)
                    if not first:
                        project_out(i - 1)
                    if last:
                        for use in range(3):
                            transposes(i, 1, use)
                        attend(i, par)
                        project_out(i)

                attention_steps(pe, half, step)

            pe.wait_ge(const_ready, 2)
            pe.wait_ge(router_w_loaded, 32)
            route(0, 0)
            prepare_weights()
            route(1, 1)
            pe.wait_ge(wt_ready, 5)
            pe.wait_ge(kq_lo_ready, HEADS // 4)
            pe.wait_ge(w1_lo_ready, 4)
            pe.wait_ge(w2_loaded, 32)
            experts(0)
            experts(1)
            for _ in transpose_tokens(2, 1):
                pass
            pe.wait_ge(tr_taken, GB * 3)
            attention(0)
            for _ in transpose_tokens(3, 1):
                pass
            pe.wait_ge(tr_taken, GB * 4)
            route(2, 4)
            attention(1)
            route(3, 5)
            experts(2)
            experts(3)


_INS = ["L0_attn_x", "L0_attn_W_Q", "L0_attn_W_K", "L0_attn_W_V", "L0_attn_W_O", "L0_ffn_Wr", "L0_ffn_br",
        "L0_ffn_W1", "L0_ffn_b1", "L0_ffn_W2", "L0_ffn_b2"]
_OUTS = [((8, 512, 128), "float32")]


def kernel(**inputs):
    import numpy as _np
    import concourse.bacc as _bacc
    from concourse import mybir as _mybir
    from concourse.bass_utils import run_bass_kernel_spmd as _run

    nc = _bacc.Bacc("TRN2", target_bir_lowering=False, num_devices=1)
    arrays, args = {}, []
    for name in _INS:
        a = _np.ascontiguousarray(inputs[name])
        arrays[f"in_{name}_dram"] = a
        args.append(nc.dram_tensor(f"in_{name}_dram", a.shape, _mybir.dt.from_np(a.dtype), kind="ExternalInput").ap())
    for i, (shape, dtype) in enumerate(_OUTS):
        dt = _mybir.dt.from_np(_np.dtype(dtype))
        args.append(nc.dram_tensor(f"out_{i}_dram", shape, dt, kind="ExternalOutput").ap())
    macaron_block_kernel(nc, *args)
    r = _run(nc, [arrays], core_ids=[0])
    return r.results[0]["out_0_dram"]
```

```python
import concourse.bass as bass
from concourse import mybir
from contextlib import ExitStack


def macaron_block_kernel(
    nc: bass.Bass,
    x: bass.AP,
    w_q: bass.AP,
    w_k: bass.AP,
    w_v: bass.AP,
    w_o: bass.AP,
    w_r: bass.AP,
    b_r: bass.AP,
    w_1: bass.AP,
    b_1: bass.AP,
    w_2: bass.AP,
    b_2: bass.AP,
    out: bass.AP,
):
    fp32 = mybir.dt.float32
    fp32r = mybir.dt.float32r
    bf16 = mybir.dt.bfloat16
    ALU = mybir.AluOpType
    ACT = mybir.ActivationFunctionType
    AX = mybir.AxisListType

    P = 128
    BATCH, SEQ, D = x.shape
    HEADS, DH, _ = w_q.shape
    TILES = BATCH * SEQ // P
    QT = SEQ // P
    PAIRS = HEADS // 2
    STEPS = BATCH * PAIRS
    EXPERTS, _, HIDDEN = w_1.shape
    CHUNKS = HIDDEN // P
    GROUPS = 2
    GB = BATCH // GROUPS
    GT = GB * QT
    TOP = 2
    UNROLL = 4
    SLOT_TILES = -(-((GT * P * TOP + EXPERTS * (P - 1)) // P) // UNROLL) * UNROLL
    assert (SLOT_TILES // UNROLL - 2) * UNROLL == TOP * GT
    assert STEPS // GROUPS == TOP * GT
    RING = 4
    INSTANCES = 2 * GROUPS
    SCALE = float(DH) ** -0.5
    EPS = 1e-5
    MASKED = -1e10

    x_tiles = x.rearrange("b (t p) d -> p (b t) d", p=P)
    out_tiles = out.rearrange("b (t p) d -> p (b t) d", p=P)

    ctx = ExitStack()
    with ctx:
        def sb(name, shape, dt=fp32):
            return ctx.enter_context(nc.sbuf_tensor(name, shape, dt))

        def sem(name):
            return ctx.enter_context(nc.semaphore(name))

        xs = sb("xs", [P, TILES, D])
        ident = sb("ident", [P, P])
        ident_bf = sb("ident_bf", [P, P], bf16)
        causal_bf = sb("causal_bf", [P, P], bf16)
        before_bf = sb("before_bf", [P, P], bf16)
        ones_bf = sb("ones_bf", [P, P], bf16)

        kq = sb("kq", [P, HEADS, 2, D], fp32r)
        wv_t = sb("wv_t", [D, PAIRS * P])
        wo_t = sb("wo_t", [P, PAIRS * D])
        w1_hi = sb("w1_hi", [D, EXPERTS * HIDDEN], fp32r)
        w1_lo = sb("w1_lo", [D, EXPERTS * HIDDEN], fp32r)
        w2_sb = sb("w2_sb", [P, EXPERTS * CHUNKS * D])
        b1_t = sb("b1_t", [P, EXPERTS * CHUNKS])
        b2_bc = sb("b2_bc", [P, EXPERTS, D])
        wr_sb = sb("wr_sb", [D, EXPERTS])
        br_bc = sb("br_bc", [P, EXPERTS])

        arena = sb("arena", [P, 8192])
        used = [0]

        def lot(columns):
            used[0] += columns
            assert used[0] <= 8192
            return arena[:, used[0] - columns:used[0]]

        wk_nat = lot(HEADS * D)[0:DH, :].rearrange("p (a e) -> p a e", a=HEADS)
        wq_nat = lot(HEADS * D)[0:DH, :].rearrange("p (a e) -> p a e", a=HEADS)
        wv_nat = lot(PAIRS * D).rearrange("p (j e) -> p j e", j=PAIRS)
        wo_nat = lot(HEADS * DH).rearrange("p (a h) -> p a h", a=HEADS)
        b1_nat = lot(P)[0:EXPERTS * CHUNKS, :]
        zeros = lot(1024)
        used[0] = 0
        probs = [lot(QT * SEQ).rearrange("p (t k) -> p t k", t=QT) for h in range(2)]
        probs_t = [lot(QT * SEQ).rearrange("p (k t) -> p k t", k=QT) for h in range(2)]
        used[0] = 0
        xg = [lot(D) for i in range(4)]
        h_sb = [lot(HIDDEN) for i in range(2)]
        h_t = [lot(HIDDEN).rearrange("p (c n) -> p c n", c=CHUNKS) for i in range(2)]
        y_sb = [lot(D) for i in range(2)]
        yg = [sb(f"yg{i}", [P, D])[:, :] for i in range(RING)]

        arena2 = sb("arena2", [P, 7 * SEQ])
        used2 = [0]

        def lot2(columns):
            used2[0] += columns
            assert used2[0] <= 7 * SEQ
            return arena2[:, used2[0] - columns:used2[0]]

        xn_st = [lot2(SEQ) for i in range(2)]
        v_sb = [lot2(SEQ).rearrange("p (t m) -> p t m", t=QT) for i in range(2)]
        inv_bc = [lot2(SEQ).rearrange("p (q t) -> p q t", t=QT) for i in range(2)]
        z_sb = lot2(SEQ)
        used2[0] = 0
        xt_r = [lot2(QT * P) for i in range(2)]
        w1_raw = sb("w1_raw", [D, EXPERTS * HIDDEN])

        def router_scratch(columns):
            wide, long = GT * EXPERTS, SLOT_TILES * EXPERTS
            return ([columns[:, n * wide:(n + 1) * wide].rearrange("p (t e) -> p t e", e=EXPERTS) for n in range(6)],
                    [columns[:, 6 * wide + n * long:6 * wide + (n + 1) * long] for n in range(2)])

        scratch = [router_scratch(lot2(6 * GT * EXPERTS + 2 * SLOT_TILES * EXPERTS))] * INSTANCES
        scratch[GROUPS] = router_scratch(w1_raw[:, GT * P:2 * GT * P])
        places_sb = sb("places_sb", [P, (GT + 1) * EXPERTS])
        xn_t = w1_raw[:, 0:GT * P]
        xn_all = [sb("xn_all0", [P, GT, D])[:, :, :],
                  w1_raw[:, GT * P:2 * GT * P].rearrange("p (t d) -> p t d", t=GT)]
        xn_hi = sb("xn_hi", [D, GT * P], fp32r)
        xn_lo = sb("xn_lo", [D, GT * P], fp32r)
        bn = sb("bn", [P, TILES, 6])
        mean = sb("mean", [P, TILES])
        half_var = sb("half_var", [P, TILES])
        rstd = sb("rstd", [P, TILES])
        ln_t = sb("ln_t", [P, TILES])

        rank = sb("rank", [P, EXPERTS])
        tile_start = sb("tile_start", [P, GT])
        upto = sb("upto", [P, EXPERTS, EXPERTS])
        tile_no = sb("tile_no", [P, SLOT_TILES])
        gate = [sb(f"gate{q}", [P, GT, TOP]) for q in range(GROUPS)]
        slot = [sb(f"slot{q}", [P, TOP, GT], mybir.dt.int32) for q in range(GROUPS)]
        expert_of = [sb(f"expert_of{q}", [P, SLOT_TILES], mybir.dt.int32) for q in range(GROUPS)]
        count_bf = sb("count_bf", [P, GT * EXPERTS], bf16)
        top = [sb(f"top{k}", [P, GT]) for k in range(4)]
        ex = sb("ex", [P, 4, EXPERTS])

        kq_st = [sb(f"kq_st{i}", [P, 2, 2, D], fp32r) for i in range(2)]
        g_whole = [[probs[h][:, 0, (1 + i) * P:(2 + i) * P] for h in range(2)] for i in range(2)]
        g_hi = [sb(f"g_hi{i}", [D, 2, SEQ], fp32r) for i in range(2)]
        g_lo = [sb(f"g_lo{i}", [D, 2, SEQ], fp32r) for i in range(2)]
        xg_hi = [g_hi[i][:, 0, 0:P] for i in range(2)]
        xg_lo = [g_lo[i][:, 0, 0:P] for i in range(2)]
        neg_max = sb("neg_max", [P, 2, QT])
        row_sum = sb("row_sum", [P, 2, QT])
        inv_sum = [sb(f"inv_sum{i}", [P, 2, QT]) for i in range(2)]
        inv_dram = nc.dram_tensor("inv_dram", [2, 2, P, QT], fp32).ap()
        x_slots = [nc.dram_tensor(f"x_slots{q}", [SLOT_TILES * P, D], fp32).ap() for q in range(GROUPS)]
        y_slots = [nc.dram_tensor(f"y_slots{q}", [SLOT_TILES * P, D], fp32).ap() for q in range(GROUPS)]

        bank = [ctx.enter_context(nc.psum_tensor(f"bank{i}", [P, 512], fp32)) for i in range(8)]

        x_loaded = [sem(f"x_loaded{q}") for q in range(GROUPS)]
        w_loaded = sem("w_loaded")
        const_ready = sem("const_ready")
        out_stored = sem("out_stored")

        kq_ps = sem("kq_ps")
        kq_hi_ready = sem("kq_hi_ready")
        kq_lo_ready = sem("kq_lo_ready")
        wt_ps = sem("wt_ps")
        wt_ready = sem("wt_ready")

        chain = sem("chain")
        xn_ready = sem("xn_ready")
        tr_ps = sem("tr_ps")
        tr_taken = sem("tr_taken")
        xnt_done = sem("xnt_done")
        w1_hi_ready = sem("w1_hi_ready")
        w1_lo_ready = sem("w1_lo_ready")
        ffn_w_loaded = sem("ffn_w_loaded")
        router_w_loaded = sem("router_w_loaded")
        zeroed = [sem(f"zeroed{q}") for q in range(GROUPS)]
        w2_loaded = sem("w2_loaded")
        zeros_ready = sem("zeros_ready")

        logits_ps = sem("logits_ps")
        delta_ready = sem("delta_ready")
        exp_delta = sem("exp_delta")
        counts_ready = sem("counts_ready")
        logits_taken = sem("logits_taken")
        places_ps = sem("places_ps")
        places_taken = sem("places_taken")
        routed = sem("routed")
        scattered = [sem(f"scattered{f}") for f in range(INSTANCES)]
        xg_loaded = [sem(f"xg_loaded{i}") for i in range(4)]
        xgt_ps = sem("xgt_ps")
        xg_hi_ready = sem("xg_hi_ready")
        xg_lo_ready = sem("xg_lo_ready")
        up_ps = sem("up_ps")
        up_ready = sem("up_ready")
        ht_ps = sem("ht_ps")
        ht_ready = sem("ht_ready")
        y_ps = sem("y_ps")
        y_ready = sem("y_ready")
        y_stored = [[sem(f"y_stored{f}_{i}") for i in range(2)] for f in range(INSTANCES)]
        gathered = [[sem(f"gathered{f}_{i}") for i in range(RING)] for f in range(INSTANCES)]
        combined = sem("combined")

        staged = [sem(f"staged{i}") for i in range(2)]
        g_ps = sem("g_ps")
        g_hi_ready = sem("g_hi_ready")
        g_lo_ready = sem("g_lo_ready")
        v_ps = sem("v_ps")
        v_ready = sem("v_ready")
        s_ps = sem("s_ps")
        max_ready = sem("max_ready")
        exp_done = sem("exp_done")
        inv_ready = sem("inv_ready")
        inv_stored = sem("inv_stored")
        inv_loaded = [sem(f"inv_loaded{i}") for i in range(2)]
        pt_ps = sem("pt_ps")
        pt_act = sem("pt_act")
        pt_dve = sem("pt_dve")
        z_ps = sem("z_ps")
        z_ready = sem("z_ready")
        o_ps = sem("o_ps")
        o_added = sem("o_added")

        def wait(engine, semaphore, value):
            if not isinstance(value, int) or value > 0:
                engine.wait_ge(semaphore, value)

        def attention_steps(engine, half, step, between=lambda: None):
            start, end = half * STEPS // GROUPS, (half + 1) * STEPS // GROUPS
            step(start, 0, True, False)
            step(start + 1, 1, False, False)
            if half > 0:
                between()
                step(start + 2, 0, False, False)
                step(start + 3, 1, False, False)
            with engine.Fori(start // 2 + (2 if half > 0 else 1), end // 2 - 1) as m:
                step(2 * m, 0, False, False)
                step(2 * m + 1, 1, False, False)
            step(end - 2, 0, False, False)
            step(end - 1, 1, False, True)

        def experts_of(engine, q, start, count):
            _, values = nc.values_load_multi_w_load_instructions(
                expert_of[q][0:1, bass.ds(start, count)], engines=[engine], min_val=0, max_val=EXPERTS - 1,
                skip_runtime_bounds_check_because="route() writes a count of experts, clamped to EXPERTS - 1")
            return values

        def ring_of(f):
            return 2 if f == 1 else RING

        def slot_tiles(engine, f, turn, between=lambda part: None):
            turn(0)
            if f == GROUPS:
                turn(1)
                between(0)
                turn(2)
                between(1)
                turn(3)
            with engine.Fori(4 if f == GROUPS else 1, SLOT_TILES // UNROLL - 1) as m:
                turn(m)
            turn(SLOT_TILES // UNROLL - 1)

        def tile_of(g, t):
            return xs[:, bass.ds(g * QT + t, 1), :].rearrange("p o d -> p (o d)")

        def seq_of(i, half):
            return i // PAIRS - half * GB

        def pair_of(i):
            return i % PAIRS

        ZERO_FILLS = SLOT_TILES // 8


        S_BANK, J_BANK, T_BANK, ZO_BANK = bank[0:3], bank[3:5], bank[5:7], bank[7]
        S_USE, S_COL, S_USES = [0, 0, 1, 2], [0, 2 * P, 0, 0], 3

        def score_tile(t, columns):
            return S_BANK[S_USE[t]][:, S_COL[t] + columns.start:S_COL[t] + columns.stop]

        R_BANKS = [bank[6], bank[5]]

        block = ctx.enter_context(nc.Block())

        @block.sync
        def _(sp):
            for q in range(GROUPS):
                tiles = slice(q * GT, (q + 1) * GT)
                sp.dma_start(xs[:, tiles, :], x_tiles[:, tiles, :]).then_inc(x_loaded[q], 16)
            sp.dma_start(wk_nat, w_k.rearrange("a h e -> h a e")).then_inc(w_loaded, 16)
            sp.dma_start(wq_nat, w_q.rearrange("a h e -> h a e")).then_inc(w_loaded, 16)
            sp.dma_start(wv_nat, w_v.rearrange("(j a) h e -> (a h) j e", a=2)).then_inc(w_loaded, 16)
            sp.dma_start(wo_nat, w_o.rearrange("a e h -> e a h")).then_inc(w_loaded, 16)

            def slots_io(f):
                q = f % GROUPS
                sp.wait_ge(scattered[f], 16 * TOP * GT)

                def load(n, u):
                    c = f * SLOT_TILES + n
                    wait(sp, xgt_ps, c - 3)
                    sp.dma_start(xg[u % 4], x_slots[q][bass.ds(n * P, P), :]).then_inc(xg_loaded[u % 4], 16)

                def store(n, u):
                    sp.wait_ge(y_ready, f * SLOT_TILES + n + 1)
                    sp.dma_start(y_slots[q][bass.ds(n * P, P), :], y_sb[u % 2]).then_inc(y_stored[f][u % 2], 16)

                for n in range(3):
                    load(n, n)

                def turn(m):
                    for u in range(UNROLL):
                        n = UNROLL * m + u
                        if not (isinstance(m, int) and n < 3):
                            store(n - 3, u + 1)
                        if not (isinstance(m, int) and n + 3 >= SLOT_TILES):
                            load(n + 3, u + 3)

                slot_tiles(sp, f, turn)
                for n in range(SLOT_TILES - 3, SLOT_TILES):
                    store(n, n)

            def attention_io(half):
                def stage(i, par):
                    wait(sp, g_ps, 2 * (i - 1))
                    wait(sp, v_ps, i - 1)
                    sp.dma_start(kq_st[par][:, :, :, :].bitcast(fp32),
                                 kq[:, bass.ds(pair_of(i) * 2, 2), :, :].bitcast(fp32)).then_inc(staged[par], 16)
                    sp.dma_start(xn_st[par][:, :], xn_t[:, bass.ds(seq_of(i, half) * SEQ, SEQ)]).then_inc(staged[par], 16)

                end = (half + 1) * STEPS // GROUPS

                def step(i, par, first, last):
                    if not (isinstance(i, int) and i + 2 >= end):
                        stage(i + 2, par)
                    sp.wait_ge(inv_ready, 2 * i + 2)
                    sp.dma_start(inv_dram[par].rearrange("h q t -> q h t"), inv_sum[par][:, :, :]).then_inc(inv_stored, 16)
                    sp.wait_ge(inv_stored, 16 * (i + 1))
                    for h in range(2):
                        sp.dma_start(
                            inv_bc[par][h * DH:(h + 1) * DH, :, :],
                            inv_dram[par, h].rearrange("q (o t) -> o q t", o=1).broadcast_to([DH, P, QT]),
                        ).then_inc(inv_loaded[par], 16)

                sp.wait_ge(kq_lo_ready, HEADS // 4)
                sp.wait_ge(xnt_done, GB * half + 1)
                if half > 0:
                    sp.wait_ge(logits_ps, GB * (GROUPS + 1))
                stage(half * STEPS // GROUPS, 0)
                stage(half * STEPS // GROUPS + 1, 1)
                sp.wait_ge(xnt_done, GB * (half + 1))
                attention_steps(sp, half, step)

            sp.wait_ge(wt_ps, 5)
            for q in range(GROUPS):
                sp.wait_ge(zeroed[q], 16 * ZERO_FILLS)
            slots_io(0)
            slots_io(1)
            attention_io(0)
            attention_io(1)
            sp.wait_ge(pt_ps, 3 * (2 * STEPS - 1))
            slots_io(2)
            slots_io(3)
            parts = [slice(0, GT)] + [slice(GT + b * QT, GT + (b + 1) * QT) for b in range(GB)]
            for tiles in parts:
                sp.wait_ge(combined, TOP * (GROUPS * GT + tiles.stop))
                sp.dma_start(out_tiles[:, tiles, :], xs[:, tiles, :]).then_inc(out_stored, 16)
            sp.wait_ge(out_stored, 16 * len(parts))

        @block.gpsimd
        def _(pool):
            pool.memset(zeros, 0.0).then_inc(zeros_ready, 1)
            pool.memset(ident[:, :], 0.0)
            pool.memset(ident_bf[:, :], 0.0)
            pool.memset(causal_bf[:, :], 0.0)
            pool.memset(before_bf[:, :], 1.0)
            pool.memset(ones_bf[:, :], 1.0)
            pool.memset(upto[:, :, :], 1.0).then_inc(const_ready, 1)
            pool.wait_ge(const_ready, 1)
            for m in (ident, ident_bf):
                pool.affine_select(out=m[:, :], in_=m[:, :], compare_op=ALU.not_equal, fill=1.0, base=0,
                                   pattern=[[-1, P]], channel_multiplier=1)
            pool.affine_select(out=causal_bf[:, :], in_=causal_bf[:, :], compare_op=ALU.is_ge, fill=MASKED, base=0,
                               pattern=[[-1, P]], channel_multiplier=1)
            pool.affine_select(out=before_bf[:, :], in_=before_bf[:, :], compare_op=ALU.is_gt, fill=0.0, base=0,
                               pattern=[[1, P]], channel_multiplier=-1)
            pool.affine_select(out=upto[:, :, :], in_=upto[:, :, :], compare_op=ALU.is_ge, fill=0.0, base=0,
                               pattern=[[1, EXPERTS], [-1, EXPERTS]], channel_multiplier=0)
            pool.iota(rank[:, :], pattern=[[-1, EXPERTS]], base=EXPERTS, channel_multiplier=0,
                      allow_small_or_imprecise_dtypes=True)
            pool.iota(tile_start[:, :], pattern=[[P, GT]], base=0, channel_multiplier=0,
                      allow_small_or_imprecise_dtypes=True)
            pool.iota(tile_no[:, :], pattern=[[1, SLOT_TILES]], base=0, channel_multiplier=0,
                      allow_small_or_imprecise_dtypes=True).then_inc(const_ready, 1)

            def scatter(f):
                q = f % GROUPS
                pool.wait_ge(routed, f + 1)
                for k in range(TOP):
                    for t in range(GT):
                        pool.indirect_dma_start(
                            out=x_slots[q][:, :], out_offset=bass.IndirectOffsetOnAxis(ap=slot[q][:, k, t:t + 1], axis=0),
                            in_=xn_all[q][:, t, :], in_offset=None).then_inc(scattered[f], 16)

            def gather(f):
                q = f % GROUPS
                for par in range(2):
                    pool.wait_ge(y_stored[f][par], 16 * SLOT_TILES // 2)
                for t in range(GT):
                    for k in range(TOP):
                        j, ring = TOP * t + k, (TOP * t + k) % ring_of(f)
                        wait(pool, combined, f * TOP * GT + j - ring_of(f) + 1)
                        pool.indirect_dma_start(
                            out=yg[ring], out_offset=None, in_=y_slots[q][:, :],
                            in_offset=bass.IndirectOffsetOnAxis(ap=slot[q][:, k, t:t + 1], axis=0),
                        ).then_inc(gathered[f][ring], 16)

            for q in range(GROUPS):
                pool.wait_ge(zeroed[q], 16 * ZERO_FILLS)
                scatter(q)
            gather(0)
            gather(1)
            scatter(2)
            scatter(3)
            gather(2)
            gather(3)

        @block.scalar
        def _(act):
            act.dma_start(wr_sb[:, :], w_r).then_inc(router_w_loaded, 16)
            act.dma_start(br_bc[:, :], b_r.rearrange("(o e) -> o e", o=1).broadcast_to([P, EXPERTS])).then_inc(router_w_loaded, 16)
            act.dma_start(b1_nat, b_1.rearrange("e (c p) -> (e c) p", p=P)).then_inc(w_loaded, 16)
            act.dma_start(w1_raw[:, :].rearrange("d (e n) -> d e n", e=EXPERTS), w_1.rearrange("e d n -> d e n")).then_inc(ffn_w_loaded, 16)
            act.wait_ge(zeros_ready, 1)
            for q in range(GROUPS):
                for n in range(ZERO_FILLS):
                    rows = x_slots[q][n * 8 * P:(n + 1) * 8 * P, :].rearrange("(p r) d -> p (r d)", p=P)
                    act.dma_start(rows, zeros).then_inc(zeroed[q], 16)
            act.dma_start(w2_sb[:, :].rearrange("p (e d) -> p e d", d=D), w_2.rearrange("e (c p) d -> p (e c) d", p=P)).then_inc(w2_loaded, 16)
            act.dma_start(b2_bc[:, :, :], b_2.rearrange("(o e) d -> o e d", o=1).broadcast_to([P, EXPERTS, D])).then_inc(w2_loaded, 16)

            def split_w1():
                act.wait_ge(ffn_w_loaded, 16)
                for n in range(4):
                    cols = slice(n * 1024, (n + 1) * 1024)
                    act.activation(w1_hi[:, cols], w1_raw[:, cols], ACT.Copy).then_inc(w1_hi_ready, 1)

            def take_for_router(f, l, banks=bank[6:8]):
                for g in range(GB):
                    act.wait_ge(tr_ps, GB * l + g + 1)
                    wait(act, logits_ps, GB * f + g - 1)
                    act.activation(xt_r[g % 2], banks[g % 2][:, :], ACT.Copy).then_inc(tr_taken, 1)

            def take_gates(f):
                act.wait_ge(delta_ready, f + 1)
                act.activation(top[3][:, :], top[2][:, :], ACT.Exp).then_inc(exp_delta, 1)

            def take_for_attention(l):
                for g in range(GB):
                    act.wait_ge(tr_ps, GB * l + g + 1)
                    cols = slice(g * SEQ, (g + 1) * SEQ)
                    act.activation(xn_hi[:, cols], bank[6 + g % 2][:, :], ACT.Copy)
                    act.activation(xn_t[:, cols], bank[6 + g % 2][:, :], ACT.Copy).then_inc(xnt_done, 1)

            def prepare_weights():
                for n in range(HEADS // 4):
                    act.wait_ge(kq_ps, n + 1)
                    act.activation(kq[:, 4 * n:4 * n + 4, 0, :], bank[n % 2][:, :].rearrange("p (a e) -> p a e", a=4),
                                   ACT.Copy, scale=SCALE).then_inc(kq_hi_ready, 1)
                for n, dst in enumerate((wv_t[:, 0:512], wv_t[:, 512:1024], wo_t[:, 0:512], wo_t[:, 512:1024])):
                    act.wait_ge(wt_ps, n + 1)
                    act.activation(dst, bank[2 + n % 2][:, :], ACT.Copy).then_inc(wt_ready, 1)
                act.wait_ge(wt_ps, 5)
                act.activation(b1_t[:, :], bank[4][:, 0:EXPERTS * CHUNKS], ACT.Copy).then_inc(wt_ready, 1)

            def experts(f):
                q = f % GROUPS
                act.wait_ge(routed, f + 1)

                def high(n, u):
                    c = f * SLOT_TILES + n
                    act.wait_ge(xgt_ps, c + 1)
                    wait(act, up_ps, c - 1)
                    act.activation(xg_hi[u % 2][:, :], bank[u % 2][:, 0:P], ACT.Copy).then_inc(xg_hi_ready, 1)

                def relu(n, u, e):
                    c = f * SLOT_TILES + n
                    act.wait_ge(ht_ps, c + 1)
                    wait(act, y_ps, c - 1)
                    for k in range(CHUNKS):
                        ins = act.activation(h_t[u % 2][:, k, :], bank[4 + u % 2][:, k * P:(k + 1) * P], ACT.Relu,
                                             bias=b1_t[:, bass.ds(e * CHUNKS + k, 1)])
                    ins.then_inc(ht_ready, 1)

                high(0, 0)

                def turn(m):
                    first = isinstance(m, int) and m == 0
                    e = experts_of(mybir.EngineType.Activation, q, 0 if first else UNROLL * m - 1,
                                   UNROLL if first else UNROLL + 1)
                    e = [None, *e] if first else e
                    for u in range(UNROLL):
                        n = UNROLL * m + u
                        if not (isinstance(m, int) and n + 1 >= SLOT_TILES):
                            high(n + 1, u + 1)
                        if not (isinstance(m, int) and n == 0):
                            relu(n - 1, u + 3, e[u])
                    if isinstance(m, int) and m == SLOT_TILES // UNROLL - 1:
                        relu(SLOT_TILES - 1, 3, e[UNROLL])

                def between(part):
                    if part == 0:
                        take_for_router(f + 1, 5, R_BANKS)
                    else:
                        take_gates(f + 1)

                slot_tiles(act, f, turn, between)

            def take_g(i, par, h):
                act.wait_ge(g_ps, 2 * i + h + 1)
                wait(act, s_ps, S_USES * (2 * (i - 2) + h + 1))
                src = J_BANK[(3 * par + h) % 2]
                act.activation(g_whole[par][h], src[:, 0:P], ACT.Copy)
                act.activation(g_hi[par][:, h, P:SEQ], src[:, P:SEQ], ACT.Copy).then_inc(g_hi_ready, 1)

            def take_v(i, par):
                act.wait_ge(v_ps, i + 1)
                wait(act, z_ps, i - 1)
                act.activation(v_sb[par][:, :, :], J_BANK[(3 * par + 2) % 2][:, :].rearrange("p (k m) -> p k m", m=P),
                               ACT.Copy).then_inc(v_ready, 1)

            def exps(i, h, tiles):
                head = 2 * i + h
                for t in tiles:
                    act.wait_ge(max_ready, QT * head + max(t + 1, 2))
                    if t == 0:
                        wait(act, pt_ps, 3 * (head - 1))
                        wait(act, inv_ready, head - 1)
                    act.activation(probs[h][:, t, 0:(t + 1) * P], score_tile(t, slice(0, (t + 1) * P)), ACT.Exp,
                                   bias=neg_max[:, h, t:t + 1], accum_out=row_sum[:, h, t:t + 1]).then_inc(exp_done, 1)

            def transposed(i, h):
                head = 2 * i + h
                act.wait_ge(pt_ps, 3 * head + 1)
                wait(act, z_ps, i)
                act.activation(probs_t[h][:, 0, :], T_BANK[h % 2][:, :], ACT.Copy).then_inc(pt_act, 1)

            def attention(half):
                start = half * STEPS // GROUPS
                take_g(start, 0, 0)
                take_g(start, 0, 1)
                take_v(start, 0)

                def step(i, par, first, last):
                    if not first:
                        transposed(i - 1, 1)
                    exps(i, 0, [0, 1, 2, 3])
                    if not last:
                        take_g(i + 1, 1 - par, 0)
                        take_g(i + 1, 1 - par, 1)
                    transposed(i, 0)
                    exps(i, 1, [0, 1, 2, 3])
                    if not last:
                        take_v(i + 1, 1 - par)
                    else:
                        transposed(i, 1)

                attention_steps(act, half, step, lambda: take_gates(2))

            take_for_router(0, 0)
            split_w1()
            take_gates(0)
            prepare_weights()
            take_for_router(1, 1)
            take_gates(1)
            experts(0)
            experts(1)
            take_for_attention(2)
            attention(0)
            take_for_router(2, 3)
            take_for_attention(4)
            attention(1)
            experts(2)
            experts(3)

        @block.vector
        def _(dve):
            chained = [0]

            def link(ins):
                chained[0] += 1
                ins.then_inc(chain, 1)
                dve.wait_ge(chain, chained[0])

            def split_w1():
                for n in range(4):
                    cols = slice(n * 1024, (n + 1) * 1024)
                    dve.wait_ge(w1_hi_ready, n + 1)
                    dve.tensor_tensor(w1_lo[:, cols], w1_raw[:, cols], w1_hi[:, cols].bitcast(fp32),
                                      ALU.subtract).then_inc(w1_lo_ready, 1)

            def split_kq():
                for n in range(HEADS // 4):
                    dve.wait_ge(kq_hi_ready, n + 1)
                    dve.scalar_tensor_tensor(
                        out=kq[:, 4 * n:4 * n + 4, 1, :], in0=bank[n % 2][:, :].rearrange("p (a e) -> p a e", a=4),
                        scalar=SCALE, in1=kq[:, 4 * n:4 * n + 4, 0, :].bitcast(fp32), op0=ALU.mult, op1=ALU.subtract,
                    ).then_inc(kq_lo_ready, 1)

            def go_on(work):
                for _ in work:
                    return

            def finish(work):
                for _ in work:
                    pass

            def measure(tiles):
                for n, t in enumerate(tiles):
                    dve.bn_stats(bn[:, t, :], xs[:, t, :])
                    if n % 2:
                        yield

            def statistics(tiles, rest=None):
                for n, t in enumerate(rest or range(tiles.start, tiles.stop)):
                    ins = dve.bn_stats(bn[:, t, :], xs[:, t, :])
                    if n % QT == QT - 1:
                        yield
                link(ins)
                yield
                dve.tensor_tensor(mean[:, tiles], bn[:, tiles, 1], bn[:, tiles, 4], ALU.add)
                dve.tensor_tensor(half_var[:, tiles], bn[:, tiles, 2], bn[:, tiles, 5], ALU.add)
                link(dve.tensor_tensor(ln_t[:, tiles], bn[:, tiles, 1], bn[:, tiles, 4], ALU.subtract))
                yield
                link(dve.tensor_tensor(ln_t[:, tiles], ln_t[:, tiles], ln_t[:, tiles], ALU.mult))
                yield
                dve.tensor_scalar(mean[:, tiles], mean[:, tiles], 0.5, None, ALU.mult)
                link(dve.tensor_scalar(half_var[:, tiles], half_var[:, tiles], -0.5 / D, -0.5 * EPS, ALU.mult, ALU.add))
                yield
                link(dve.scalar_tensor_tensor(out=half_var[:, tiles], in0=ln_t[:, tiles], scalar=-0.125, in1=half_var[:, tiles],
                                              op0=ALU.mult, op1=ALU.add))
                yield
                link(dve.tensor_scalar(ln_t[:, tiles], half_var[:, tiles], -2.0, None, ALU.mult))
                yield
                link(dve.tensor_scalar(rstd[:, tiles].bitcast(mybir.dt.int32), ln_t[:, tiles].bitcast(mybir.dt.int32), 1, None,
                                       ALU.logical_shift_right))
                yield
                link(dve.tensor_scalar(rstd[:, tiles].bitcast(mybir.dt.int32), rstd[:, tiles].bitcast(mybir.dt.int32), -1.0,
                                       float(0x5F3759DF), ALU.mult, ALU.add))
                yield
                for _ in range(3):
                    link(dve.tensor_tensor(ln_t[:, tiles], rstd[:, tiles], rstd[:, tiles], ALU.mult))
                    yield
                    link(dve.tensor_tensor(ln_t[:, tiles], ln_t[:, tiles], half_var[:, tiles], ALU.mult))
                    yield
                    link(dve.scalar_tensor_tensor(out=rstd[:, tiles], in0=ln_t[:, tiles], scalar=1.5, in1=rstd[:, tiles],
                                                  op0=ALU.add, op1=ALU.mult))
                    yield

            def normalise(q, buffer, split_after=None):
                def normalise_block(b):
                    for t in range(QT):
                        i = b * QT + t
                        at = q * GT + i
                        ins = dve.tensor_scalar(xn_all[buffer][:, i, :], xs[:, at, :], mean[:, at:at + 1],
                                                rstd[:, at:at + 1], ALU.subtract, ALU.mult)
                        if t % 2 == 0:
                            yield
                    ins.then_inc(xn_ready, 1)

                def split_block(g):
                    cols = slice(g * SEQ, (g + 1) * SEQ)
                    dve.wait_ge(xnt_done, split_after + g + 1)
                    dve.tensor_tensor(xn_lo[:, cols], bank[6 + g % 2][:, :], xn_hi[:, cols].bitcast(fp32),
                                      ALU.subtract).then_inc(tr_taken, 1)

                for b in range(GB):
                    yield from normalise_block(b)
                    if split_after is not None and b > 0:
                        split_block(b - 1)
                if split_after is not None:
                    split_block(GB - 1)

            def layer_norm(q, buffer, split_after=None):
                yield from statistics(slice(q * GT, (q + 1) * GT))
                yield from normalise(q, buffer, split_after)

            over_e = [P, GT, EXPERTS]

            def wide(per_token):
                return per_token.rearrange("p (t o) -> p t o", o=1).broadcast_to(over_e)

            def per_expert(row):
                return row.rearrange("p (o e) -> p o e", o=1).broadcast_to(over_e)

            def take_logits(f, logits=bank[5]):
                dve.wait_ge(logits_ps, GB * (f + 1))
                dve.tensor_tensor(scratch[f][0][0], logits[:, 0:GT * EXPERTS].rearrange("p (t e) -> p t e", e=EXPERTS),
                                  per_expert(br_bc[:, :]), ALU.add).then_inc(logits_taken, 1)

            def choose(f):
                logit, a, b, hot1, hot2, _ = scratch[f][0]
                m1, k1, delta, _ = top
                dve.wait_ge(logits_taken, f + 1)

                def hottest(values, largest, hot):
                    link(dve.tensor_reduce(largest, values, AX.X, ALU.max))
                    yield
                    link(dve.tensor_tensor(b, values, wide(largest), ALU.is_equal))
                    yield
                    link(dve.tensor_tensor(b, b, per_expert(rank[:, :]), ALU.mult))
                    yield
                    link(dve.tensor_reduce(k1[:, :], b, AX.X, ALU.max))
                    yield
                    link(dve.tensor_tensor(hot, per_expert(rank[:, :]), wide(k1[:, :]), ALU.is_equal))
                    yield

                yield from hottest(logit, m1[:, :], hot1)
                link(dve.scalar_tensor_tensor(out=a, in0=hot1, scalar=-3e38, in1=logit, op0=ALU.mult, op1=ALU.add))
                yield
                yield from hottest(a, delta[:, :], hot2)
                dve.tensor_tensor(count_bf[:, :].rearrange("p (t e) -> p t e", e=EXPERTS), hot1, hot2,
                                  ALU.add).then_inc(counts_ready, 1)
                dve.tensor_tensor(delta[:, :], delta[:, :], m1[:, :], ALU.subtract).then_inc(delta_ready, 1)

            def take_places(f, counts):
                dve.wait_ge(places_ps, f + 1)
                dve.tensor_copy(places_sb[:, :], counts[:, 0:(GT + 1) * EXPERTS]).then_inc(places_taken, 1)

            def place_tokens(f):
                q = f % GROUPS
                (_, a, _, hot1, hot2, place), rt2 = scratch[f]
                _, k1, _, e_delta = top
                dve.wait_ge(exp_delta, f + 1)
                link(dve.tensor_scalar(k1[:, :], e_delta[:, :], 1.0, 2.0, ALU.add, ALU.mult))
                yield
                link(dve.reciprocal(gate[q][:, :, 0], k1[:, :]))
                yield
                dve.tensor_tensor(gate[q][:, :, 1], gate[q][:, :, 0], e_delta[:, :], ALU.mult)

                dve.wait_ge(places_taken, f + 1)
                placed = places_sb[:, 0:GT * EXPERTS].rearrange("p (t e) -> p t e", e=EXPERTS)
                number, tiles, ends, base = (ex[:, i, :] for i in range(4))
                link(dve.tensor_copy(number, places_sb[:, GT * EXPERTS:]))
                yield
                over = rt2[0][:, 0:EXPERTS * GT].rearrange("p (e j) -> p e j", j=GT)
                link(dve.tensor_tensor(over, number.rearrange("p (e o) -> p e o", o=1).broadcast_to([P, EXPERTS, GT]),
                                       tile_start[:, :].rearrange("p (o j) -> p o j", o=1).broadcast_to([P, EXPERTS, GT]),
                                       ALU.is_gt))
                yield
                link(dve.tensor_reduce(tiles, over, AX.X, ALU.add))
                yield
                sums = rt2[0][:, 0:EXPERTS * EXPERTS].rearrange("p (e g) -> p e g", g=EXPERTS)
                link(dve.tensor_tensor(sums, upto[:, :, :],
                                       tiles.rearrange("p (o g) -> p o g", o=1).broadcast_to([P, EXPERTS, EXPERTS]),
                                       ALU.mult))
                yield
                link(dve.tensor_reduce(ends, sums, AX.X, ALU.add))
                yield
                link(dve.tensor_tensor(base, ends, tiles, ALU.subtract))
                yield
                link(dve.tensor_scalar(base, base, float(P), None, ALU.mult))
                yield
                link(dve.tensor_tensor(place, placed, per_expert(base), ALU.add))
                yield
                for k, hot in enumerate((hot1, hot2)):
                    link(dve.tensor_tensor(a, place, hot, ALU.mult))
                    yield
                    link(dve.tensor_reduce(k1[:, :], a, AX.X, ALU.add))
                    yield
                    link(dve.tensor_copy(slot[q][:, k, :], k1[:, :]))
                    yield
                ended = rt2[1].rearrange("p (n e) -> p n e", e=EXPERTS)
                link(dve.tensor_tensor(ended, tile_no[:, :].rearrange("p (n o) -> p n o", o=1).broadcast_to([P, SLOT_TILES, EXPERTS]),
                                       ends.rearrange("p (o e) -> p o e", o=1).broadcast_to([P, SLOT_TILES, EXPERTS]),
                                       ALU.is_ge))
                yield
                link(dve.tensor_reduce(rt2[0][:, 0:SLOT_TILES], ended, AX.X, ALU.add))
                yield
                dve.tensor_scalar(expert_of[q][:, :], rt2[0][:, 0:SLOT_TILES], float(EXPERTS - 1), None,
                                  ALU.min).then_inc(routed, 1)

            def route(f):
                take_logits(f)
                finish(choose(f))
                take_places(f, bank[5])
                finish(place_tokens(f))

            def experts(f, combining=None):
                q = f % GROUPS

                def low(n, u):
                    c = f * SLOT_TILES + n
                    dve.wait_ge(xg_hi_ready, c + 1)
                    wait(dve, up_ps, c - 1)
                    dve.tensor_tensor(xg_lo[u % 2][:, :], bank[u % 2][:, 0:P], xg_hi[u % 2][:, :].bitcast(fp32),
                                      ALU.subtract).then_inc(xg_lo_ready, 1)

                def take_up(n, u):
                    c = f * SLOT_TILES + n
                    dve.wait_ge(up_ps, c + 1)
                    wait(dve, ht_ps, c - 1)
                    dve.tensor_copy(h_sb[u % 2], bank[2 + u % 2][:, :]).then_inc(up_ready, 1)

                def take_y(n, u, e):
                    c = f * SLOT_TILES + n
                    dve.wait_ge(y_ps, c + 1)
                    wait(dve, y_stored[f][u % 2], 16 * (n // 2))
                    dve.tensor_tensor(y_sb[u % 2], bank[6 + u % 2][:, 0:P],
                                      b2_bc[:, bass.ds(e, 1), :].rearrange("p o d -> p (o d)"), ALU.add).then_inc(y_ready, 1)

                work = layer_norm(1, 1) if f == GROUPS else iter(())

                def between(part):
                    nonlocal work
                    finish(work)
                    if part == 0:
                        take_logits(f + 1, bank[1])
                        work = choose(f + 1)
                    else:
                        take_places(f + 1, bank[1])
                        work = place_tokens(f + 1)

                dve.wait_ge(routed, f + 1)
                if f > 0:
                    for par in range(2):
                        dve.wait_ge(y_stored[f - 1][par], 16 * SLOT_TILES // 2)
                low(0, 0)

                def turn(m):
                    nonlocal work
                    if f == 1 and isinstance(m, int) and m > 0:
                        dve.wait_ge(combined, TOP * GT)
                        work = measure(range(GT - 1))
                    first = isinstance(m, int) and m == 0
                    e = experts_of(mybir.EngineType.DVE, q, 0 if first else UNROLL * m - 2,
                                   UNROLL if first else UNROLL + 2)
                    e = [None, None, *e] if first else e
                    for u in range(UNROLL):
                        n = UNROLL * m + u
                        if not (isinstance(m, int) and n + 1 >= SLOT_TILES):
                            low(n + 1, u + 1)
                        go_on(work)
                        take_up(n, u)
                        go_on(work)
                        if not (isinstance(m, int) and n < 2):
                            take_y(n - 2, u + 2, e[u])
                        go_on(work)
                        if combining is not None and not isinstance(m, int):
                            combine(combining, (m - 1) * (UNROLL // TOP) + u // TOP, u % TOP, u, m)
                    if isinstance(m, int) and m == SLOT_TILES // UNROLL - 1:
                        take_y(SLOT_TILES - 2, 2, e[UNROLL])
                        take_y(SLOT_TILES - 1, 3, e[UNROLL + 1])
                    if isinstance(m, int) and m >= 3:
                        finish(work)

                slot_tiles(dve, f, turn, between)

            def combine(f, t, k, ring, use):
                q = f % GROUPS
                dve.wait_ge(gathered[f][ring], 16 * use)
                if k > 0:
                    dve.wait_ge(combined, f * TOP * GT + TOP * t + k)
                tokens = tile_of(q * GB, t)
                dve.scalar_tensor_tensor(
                    out=tokens, in0=yg[ring], scalar=gate[q][:, bass.ds(t, 1), k], in1=tokens,
                    op0=ALU.mult, op1=ALU.add).then_inc(combined, 1)

            def combine_all(f):
                def tiles(b):
                    for s in range(RING):
                        combine(f, b * (RING // TOP) + s // TOP, s % TOP, s, b + 1)

                tiles(0)
                with dve.Fori(1, TOP * GT // RING) as b:
                    tiles(b)

            def take_g(i, par, h):
                dve.wait_ge(g_hi_ready, 2 * i + h + 1)
                wait(dve, s_ps, S_USES * (2 * (i - 2) + h + 1))
                dve.tensor_tensor(g_lo[par][:, h, P:SEQ], J_BANK[(3 * par + h) % 2][:, P:SEQ],
                                  g_hi[par][:, h, P:SEQ].bitcast(fp32), ALU.subtract).then_inc(g_lo_ready, 1)

            def maxima(i, h):
                head = 2 * i + h
                for t in range(QT):
                    dve.wait_ge(s_ps, S_USES * head + S_USE[t] + 1)
                    if t == 0:
                        wait(dve, exp_done, QT * (head - 1))
                    dve.tensor_reduce(neg_max[:, h, t:t + 1], score_tile(t, slice(0, (t + 1) * P)), AX.X, ALU.max,
                                      negate=True).then_inc(max_ready, 1)

            def invert(i, h, par):
                head = 2 * i + h
                dve.wait_ge(exp_done, QT * (head + 1))
                wait(dve, inv_stored, 16 * (i - 1))
                if h == 1:
                    wait(dve, z_ready, i - 1)
                dve.reciprocal(inv_sum[par][:, h, :], row_sum[:, h, :]).then_inc(inv_ready, 1)

            def transposed(i, h, use):
                head = 2 * i + h
                dve.wait_ge(pt_ps, 3 * head + use + 1)
                wait(dve, z_ps, i)
                src = T_BANK[(h + use) % 2]
                if use == 1:
                    dve.tensor_copy(probs_t[h][:, 1, P:SEQ], src[:, 0:3 * P]).then_inc(pt_dve, 1)
                else:
                    dve.tensor_copy(probs_t[h][:, 2, 2 * P:SEQ], src[:, 0:2 * P])
                    dve.tensor_copy(probs_t[h][:, 3, 3 * P:SEQ], src[:, 2 * P:3 * P]).then_inc(pt_dve, 1)

            def divide_by_sums(i, par):
                dve.wait_ge(z_ps, i + 1)
                dve.wait_ge(inv_loaded[par], 32 * (i // 2 + 1))
                wait(dve, o_ps, i)
                dve.tensor_tensor(z_sb[:, :].rearrange("p (t q) -> p t q", t=QT),
                                  ZO_BANK[:, :].rearrange("p (t q) -> p t q", t=QT),
                                  inv_bc[par][:, :, :].rearrange("p q t -> p t q"), ALU.mult).then_inc(z_ready, 1)

            def add_out(i, half):
                dve.wait_ge(o_ps, i + 1)
                wait(dve, o_added, i)
                tokens = xs[:, bass.ds((i // PAIRS) * QT, QT), :]
                dve.tensor_tensor(tokens, ZO_BANK[:, :].rearrange("p (t d) -> p t d", t=QT), tokens,
                                  ALU.add).then_inc(o_added, 1)

            def attention(half, combining=None):
                start = half * STEPS // GROUPS
                take_g(start, 0, 0)
                take_g(start, 0, 1)

                f = GROUPS + half - 1
                work = choose(f) if half > 0 else iter(())

                def between():
                    nonlocal work
                    finish(work)
                    take_places(f, T_BANK[1])
                    work = place_tokens(f)

                def step(i, par, first, last):
                    nonlocal work
                    if half == 0 and isinstance(i, int) and i == STEPS // GROUPS - 2:
                        dve.wait_ge(o_added, (GB - 1) * PAIRS)
                        dve.wait_ge(combined, TOP * (TILES - 1))
                        work = measure([*range(GT - QT), *range(GT, TILES - 1)])
                    maxima(i, 0)
                    go_on(work)
                    if not first:
                        transposed(i - 1, 1, 1)
                        go_on(work)
                    if combining is not None:
                        combine(combining, i // TOP, par, par, i // TOP + 1)
                    if not first:
                        transposed(i - 1, 1, 2)
                        go_on(work)
                    if not last:
                        take_g(i + 1, 1 - par, 0)
                        go_on(work)
                        take_g(i + 1, 1 - par, 1)
                        go_on(work)
                    invert(i, 0, par)
                    if not first:
                        divide_by_sums(i - 1, 1 - par)
                        go_on(work)
                    maxima(i, 1)
                    go_on(work)
                    transposed(i, 0, 1)
                    go_on(work)
                    transposed(i, 0, 2)
                    invert(i, 1, par)
                    go_on(work)
                    if isinstance(i, int) and i == start + 3 or last:
                        finish(work)
                    if not first:
                        add_out(i - 1, half)
                    if last:
                        transposed(i, 1, 1)
                        transposed(i, 1, 2)
                        divide_by_sums(i, par)
                        add_out(i, half)

                attention_steps(dve, half, step, between)

            dve.wait_ge(x_loaded[0], 16)
            finish(layer_norm(0, 0))
            dve.wait_ge(router_w_loaded, 32)
            dve.wait_ge(const_ready, 2)
            route(0)
            split_w1()
            split_kq()
            dve.wait_ge(w1_lo_ready, 4)
            dve.wait_ge(x_loaded[1], 16)
            finish(layer_norm(1, 1))
            route(1)
            dve.wait_ge(w2_loaded, 32)
            experts(0)
            experts(1, combining=0)
            dve.wait_ge(scattered[1], 16 * TOP * GT)
            dve.wait_ge(combined, TOP * GT)
            finish(statistics(slice(0, GT), rest=range(GT - 1, GT)))
            finish(normalise(0, 1, split_after=0))
            attention(0, combining=1)
            dve.wait_ge(combined, TOP * GT * 2)
            dve.wait_ge(o_added, STEPS // 2)
            finish(statistics(slice(0, TILES), rest=[*range(GT - QT, GT), TILES - 1]))
            finish(normalise(0, 0))
            finish(normalise(1, 1, split_after=GB))
            take_logits(2)
            attention(1)
            dve.wait_ge(o_added, STEPS)
            experts(2)
            experts(3, combining=2)
            combine_all(3)

        @block.tensor
        def _(pe):
            def transpose_tokens(l, buffer, banks=bank[6:8]):
                for g in range(GB):
                    pe.wait_ge(xn_ready, GB * l + g + 1)
                    wait(pe, tr_taken, GB * l + g - 1)
                    for t in range(QT):
                        ins = pe.transpose(banks[g % 2][:, t * P:(t + 1) * P], xn_all[buffer][:, g * QT + t, :],
                                           ident[:, :])
                    ins.then_inc(tr_ps, 1)
                    yield g

            def route(f, l, out=bank[5], banks=bank[6:8]):
                q = f % GROUPS

                def logits(g):
                    pe.wait_ge(tr_taken, GB * l + g + 1)
                    for t in range(QT):
                        at = (g * QT + t) * EXPERTS
                        ins = pe.matmul(out[:, at:at + EXPERTS], xt_r[g % 2][:, t * P:(t + 1) * P], wr_sb[:, :],
                                        start=True, stop=True)
                    ins.then_inc(logits_ps, 1)

                for g in transpose_tokens(l, q, banks):
                    if g > 0:
                        logits(g - 1)
                logits(GB - 1)

            def count(f, counts):
                pe.wait_ge(counts_ready, f + 1)
                width = GT * EXPERTS
                pe.matmul(counts[:, 0:width], before_bf[:, :], count_bf[:, :], start=True, stop=False)
                for t in range(1, GT):
                    pe.matmul(counts[:, t * EXPERTS:width], ones_bf[:, :], count_bf[:, 0:width - t * EXPERTS],
                              start=False, stop=(t == GT - 1))
                for t in range(GT):
                    ins = pe.matmul(counts[:, width:width + EXPERTS], ones_bf[:, :],
                                    count_bf[:, t * EXPERTS:(t + 1) * EXPERTS], start=(t == 0), stop=(t == GT - 1))
                ins.then_inc(places_ps, 1)

            def prepare_weights():
                pe.wait_ge(w_loaded, 80)
                for n in range(HEADS // 4):
                    wait(pe, kq_lo_ready, n - 1)
                    for a in range(4):
                        ins = pe.matmul(bank[n % 2][:, a * D:(a + 1) * D], wk_nat[:, 4 * n + a, :],
                                        wq_nat[:, 4 * n + a, :], start=True, stop=True)
                    ins.then_inc(kq_ps, 1)
                for n in range(4):
                    wait(pe, wt_ready, n - 1)
                    for a in range(4):
                        j = 4 * (n % 2) + a
                        src = wv_nat[:, j, :] if n < 2 else wo_nat[:, 2 * j:2 * j + 2, :].rearrange("e a h -> e (a h)")
                        ins = pe.transpose(bank[2 + n % 2][:, a * P:(a + 1) * P], src, ident[:, :])
                    ins.then_inc(wt_ps, 1)
                rows = EXPERTS * CHUNKS
                pe.transpose(bank[4][:, 0:rows], b1_nat, ident[0:rows, 0:rows]).then_inc(wt_ps, 1)

            def experts(f):
                q = f % GROUPS
                pe.wait_ge(routed, f + 1)
                pe.wait_ge(tr_taken, GB * 2)

                def transpose_x(n, u):
                    c = f * SLOT_TILES + n
                    pe.wait_ge(xg_loaded[u % 4], 16 * (f * SLOT_TILES // 4 + n // 4 + 1))
                    wait(pe, xg_lo_ready, c - 1)
                    pe.transpose(bank[u % 2][:, 0:P], xg[u % 4], ident[:, :]).then_inc(xgt_ps, 1)

                def up(n, u, e):
                    c = f * SLOT_TILES + n
                    cols = bass.ds(e * HIDDEN, HIDDEN)
                    pe.wait_ge(xg_lo_ready, c + 1)
                    wait(pe, up_ready, c - 1)
                    dst = bank[2 + u % 2][:, :]
                    pe.matmul(dst, xg_lo[u % 2][:, :], w1_hi[:, cols], start=True, stop=False)
                    pe.matmul(dst, xg_hi[u % 2][:, :], w1_lo[:, cols], start=False, stop=False)
                    pe.matmul(dst, xg_hi[u % 2][:, :], w1_hi[:, cols], start=False, stop=True).then_inc(up_ps, 1)

                def transpose_h(n, u):
                    c = f * SLOT_TILES + n
                    pe.wait_ge(up_ready, c + 1)
                    wait(pe, ht_ready, c - 1)
                    for k in range(CHUNKS):
                        ins = pe.transpose(bank[4 + u % 2][:, k * P:(k + 1) * P], h_sb[u % 2][:, k * P:(k + 1) * P],
                                           ident[:, :])
                    ins.then_inc(ht_ps, 1)

                def down(n, u, e):
                    c = f * SLOT_TILES + n
                    pe.wait_ge(ht_ready, c + 1)
                    wait(pe, y_ready, c - 1)
                    for k in range(CHUNKS):
                        ins = pe.matmul(bank[6 + u % 2][:, 0:P], h_t[u % 2][:, k, :],
                                        w2_sb[:, bass.ds(e * (CHUNKS * D) + k * D, D)],
                                        start=(k == 0), stop=(k == CHUNKS - 1))
                    ins.then_inc(y_ps, 1)

                transpose_x(0, 0)

                def turn(m):
                    first = isinstance(m, int) and m == 0
                    e = experts_of(mybir.EngineType.PE, q, 0 if first else UNROLL * m - 2,
                                   UNROLL if first else UNROLL + 2)
                    e = [None, None, *e] if first else e
                    for u in range(UNROLL):
                        n = UNROLL * m + u
                        if not (isinstance(m, int) and n + 1 >= SLOT_TILES):
                            if f == GROUPS and isinstance(m, int) and n == 2 * UNROLL:
                                pe.wait_ge(logits_taken, f + 2)
                            if f == GROUPS and isinstance(m, int) and n == 3 * UNROLL:
                                pe.wait_ge(places_taken, f + 2)
                            transpose_x(n + 1, u + 1)
                        up(n, u, e[u + 2])
                        if not (isinstance(m, int) and n < 1):
                            transpose_h(n - 1, u + 3)
                        if not (isinstance(m, int) and n < 2):
                            down(n - 2, u + 2, e[u])
                    if isinstance(m, int) and m == SLOT_TILES // UNROLL - 1:
                        transpose_h(SLOT_TILES - 1, 3)
                        down(SLOT_TILES - 2, 2, e[UNROLL])
                        down(SLOT_TILES - 1, 3, e[UNROLL + 1])

                def between(part):
                    done = f * SLOT_TILES + (2 + part) * UNROLL
                    pe.wait_ge(xg_lo_ready, done)
                    if part == 0:
                        pe.wait_ge(y_ready, done - 3)
                        pe.wait_ge(ht_ready, done - 2)
                        route(f + 1, 5, bank[1], R_BANKS)
                    else:
                        count(f + 1, bank[1])

                slot_tiles(pe, f, turn, between)

            def project_g(i, par, h, half):
                cols = bass.ds(seq_of(i, half) * SEQ, SEQ)
                if h == 0:
                    pe.wait_ge(staged[par], 32 * (i // 2 + 1))
                    wait(pe, g_lo_ready, 2 * i)
                else:
                    wait(pe, v_ready, i)
                dst = J_BANK[(3 * par + h) % 2][:, :]
                pe.matmul(dst, kq_st[par][:, h, 1, :], xn_hi[:, cols], start=True, stop=False)
                pe.matmul(dst, kq_st[par][:, h, 0, :], xn_lo[:, cols], start=False, stop=False)
                pe.matmul(dst, kq_st[par][:, h, 0, :], xn_hi[:, cols], start=False, stop=True).then_inc(g_ps, 1)

            def project_v(i, par):
                pe.wait_ge(g_lo_ready, 2 * i + 1)
                dst = J_BANK[(3 * par + 2) % 2]
                for k in range(QT):
                    ins = pe.matmul(dst[:, k * P:(k + 1) * P], xn_st[par][:, k * P:(k + 1) * P],
                                    wv_t[:, bass.ds(pair_of(i) * P, P)], start=True, stop=True)
                ins.then_inc(v_ps, 1)

            def scores(i, h, par, tiles, half):
                head = 2 * i + h
                for t in tiles:
                    if t == 0:
                        pe.wait_ge(g_lo_ready, head + 1)
                    if t != 1:
                        wait(pe, exp_done, QT * (head - 1) + max(t + 1, 2))
                    cols = bass.ds(seq_of(i, half) * SEQ, (t + 1) * P)
                    q = slice(t * P, (t + 1) * P)
                    dst = score_tile(t, slice(0, (t + 1) * P))
                    if t == 0:
                        pe.matmul(dst, g_whole[par][h], xn_t[:, cols], start=True, stop=False)
                    else:
                        pe.matmul(dst, g_lo[par][:, h, q], xn_hi[:, cols], start=True, stop=False)
                        pe.matmul(dst, g_hi[par][:, h, q], xn_lo[:, cols], start=False, stop=False)
                        pe.matmul(dst, g_hi[par][:, h, q], xn_hi[:, cols], start=False, stop=False)
                    ins = pe.matmul(score_tile(t, q), ident_bf[:, :], causal_bf[:, :], start=False, stop=True)
                    if t > 0:
                        ins.then_inc(s_ps, 1)

            def transposes(i, h, use):
                head = 2 * i + h
                src = probs[h]
                dst = T_BANK[(h + use) % 2]
                if use == 0:
                    pe.wait_ge(exp_done, QT * (head + 1))
                    wait(pe, pt_dve, 2 * head - 1)
                    for t in range(QT):
                        ins = pe.transpose(dst[:, t * P:(t + 1) * P], src[:, t, 0:P], ident[:, :])
                if use == 1:
                    wait(pe, pt_dve, 2 * head)
                    for t in range(1, QT):
                        ins = pe.transpose(dst[:, (t - 1) * P:t * P], src[:, t, P:2 * P], ident[:, :])
                if use == 2:
                    pe.wait_ge(pt_act, head + 1)
                    pe.transpose(dst[:, 0:P], src[:, 2, 2 * P:3 * P], ident[:, :])
                    pe.transpose(dst[:, P:2 * P], src[:, 3, 2 * P:3 * P], ident[:, :])
                    ins = pe.transpose(dst[:, 2 * P:3 * P], src[:, 3, 3 * P:4 * P], ident[:, :])
                ins.then_inc(pt_ps, 1)

            def attend(i, par):
                pe.wait_ge(v_ready, i + 1)
                pe.wait_ge(pt_act, 2 * i + 2)
                wait(pe, o_added, i)
                for k in range(QT):
                    if k in (1, 2):
                        pe.wait_ge(pt_dve, 4 * i + 2 + k)
                    for h in range(2):
                        m = slice(h * DH, (h + 1) * DH)
                        ins = pe.matmul(ZO_BANK[m, k * P:SEQ], v_sb[par][:, k, m], probs_t[h][:, k, k * P:SEQ],
                                        start=(k == 0), stop=(k == QT - 1))
                ins.then_inc(z_ps, 1)

            def project_out(i):
                pe.wait_ge(z_ready, i + 1)
                for t in range(QT):
                    ins = pe.matmul(ZO_BANK[:, t * D:(t + 1) * D], z_sb[:, t * P:(t + 1) * P],
                                    wo_t[:, bass.ds(pair_of(i) * D, D)], start=True, stop=True)
                ins.then_inc(o_ps, 1)

            def attention(half, taken):
                start = half * STEPS // GROUPS
                pe.wait_ge(tr_taken, taken - GB + 1)
                project_g(start, 0, 0, half)
                project_g(start, 0, 1, half)
                project_v(start, 0)
                pe.wait_ge(tr_taken, taken)
                pe.wait_ge(logits_taken, GROUPS + half)

                def step(i, par, first, last):
                    scores(i, 0, par, [0, 1, 2], half)
                    if half > 0 and isinstance(i, int) and i == start + 2:
                        pe.wait_ge(places_taken, GROUPS + half)
                    if not first:
                        transposes(i - 1, 1, 0)
                    scores(i, 0, par, [3], half)
                    if not first:
                        transposes(i - 1, 1, 1)
                    if not last:
                        project_g(i + 1, 1 - par, 0, half)
                    if not first:
                        transposes(i - 1, 1, 2)
                    if not last:
                        project_g(i + 1, 1 - par, 1, half)
                    if not first:
                        attend(i - 1, 1 - par)
                    scores(i, 1, par, [0, 1, 2], half)
                    transposes(i, 0, 0)
                    scores(i, 1, par, [3], half)
                    transposes(i, 0, 1)
                    if not last:
                        project_v(i + 1, 1 - par)
                    transposes(i, 0, 2)
                    if not first:
                        project_out(i - 1)
                    if last:
                        for use in range(3):
                            transposes(i, 1, use)
                        attend(i, par)
                        project_out(i)

                def between():
                    pe.wait_ge(pt_dve, 4 * (start + 1) + 1)
                    count(GROUPS + half - 1, T_BANK[1])

                attention_steps(pe, half, step, between)

            pe.wait_ge(const_ready, 2)
            pe.wait_ge(router_w_loaded, 32)
            route(0, 0)
            count(0, bank[5])
            prepare_weights()
            route(1, 1)
            count(1, bank[5])
            pe.wait_ge(wt_ready, 5)
            pe.wait_ge(kq_lo_ready, HEADS // 4)
            pe.wait_ge(w1_lo_ready, 4)
            pe.wait_ge(w2_loaded, 32)
            experts(0)
            experts(1)
            for _ in transpose_tokens(2, 1):
                pass
            attention(0, GB * 3)
            route(2, 3)
            for _ in transpose_tokens(4, 1):
                pass
            attention(1, GB * 5)
            experts(2)
            experts(3)


_INS = ["L0_attn_x", "L0_attn_W_Q", "L0_attn_W_K", "L0_attn_W_V", "L0_attn_W_O", "L0_ffn_Wr", "L0_ffn_br",
        "L0_ffn_W1", "L0_ffn_b1", "L0_ffn_W2", "L0_ffn_b2"]
_OUTS = [((8, 512, 128), "float32")]


def kernel(**inputs):
    import numpy as _np
    import concourse.bacc as _bacc
    from concourse import mybir as _mybir
    from concourse.bass_utils import run_bass_kernel_spmd as _run

    nc = _bacc.Bacc("TRN2", target_bir_lowering=False, num_devices=1)
    arrays, args = {}, []
    for name in _INS:
        a = _np.ascontiguousarray(inputs[name])
        arrays[f"in_{name}_dram"] = a
        args.append(nc.dram_tensor(f"in_{name}_dram", a.shape, _mybir.dt.from_np(a.dtype), kind="ExternalInput").ap())
    for i, (shape, dtype) in enumerate(_OUTS):
        dt = _mybir.dt.from_np(_np.dtype(dtype))
        args.append(nc.dram_tensor(f"out_{i}_dram", shape, dt, kind="ExternalOutput").ap())
    macaron_block_kernel(nc, *args)
    r = _run(nc, [arrays], core_ids=[0])
    return r.results[0]["out_0_dram"]
```
